# Optimizing a Trainium2 kernel written in Bass

```python
import numpy as np
import jax
import jax.numpy as jnp

def _softmax(x, axis=-1):
    return jax.nn.softmax(x, axis=axis)

def _gelu(x):
    return jax.nn.gelu(x, approximate=True)

def _silu(x):
    return jax.nn.silu(x)

def _sigmoid(x):
    return jax.nn.sigmoid(x)

def _layernorm(x, axis=-1, eps=1e-05):
    m = jnp.mean(x, axis=axis, keepdims=True)
    v = jnp.var(x, axis=axis, keepdims=True)
    return (x - m) / jnp.sqrt(v + eps)

def _scatter_add(tgt, idx, src, axis=0):
    return tgt.at[idx].add(src)

def _segment_sum(src, seg, n):
    return jax.ops.segment_sum(src, seg, n)
kernel_name = 'mk_gnn_preln_d4_gnn_r32_db1a64'

def setup_inputs(seed: int=0):
    np.random.seed(seed)
    _w = jnp.asarray

    def _rec_inputs():
        import jax
        import jax.numpy as jnp
        _gk = jax.random.key(seed)
        x = -0.0002117 + 1 * jax.random.normal(jax.random.fold_in(_gk, 1), (3125, 256), jnp.float32)
        _s = jax.random.randint(jax.random.fold_in(_gk, 2), (25000,), 0, 3125, jnp.int32)
        _d = jax.random.randint(jax.random.fold_in(_gk, 3), (25000,), 0, 3125, jnp.int32)
        _loop = jnp.arange(3125, dtype=jnp.int32)
        src = jnp.concatenate([_s, _d, _loop])
        dst = jnp.concatenate([_d, _s, _loop])
        _o = jnp.argsort(dst, stable=True)
        src = src[_o]
        dst = dst[_o]
        edge_attr_3 = -1.09012e-05 + 0.99985 * jax.random.normal(jax.random.fold_in(_gk, 11), (53125, 3), jnp.float32)
        edge_type_3 = jax.random.randint(jax.random.fold_in(_gk, 13), (53125,), 0, 3, jnp.int32)
        edge_weight = jax.random.uniform(jax.random.fold_in(_gk, 14), (53125,), jnp.float32, 0.0, 0.999999)
        node_type_4 = jax.random.randint(jax.random.fold_in(_gk, 15), (3125,), 0, 4, jnp.int32)
        return (x, src, dst, edge_attr_3, edge_type_3, edge_weight, node_type_4)
    x, src, dst, edge_attr_3, edge_type_3, edge_weight, node_type_4 = _rec_inputs()

    def _L0_gnn_setup():
        import jax, jax.numpy as jnp
        import numpy as np
        N_NODES = 3125
        N_EDGES = 50000
        D = 256
        key = jax.random.key(seed)
        ks = jax.random.split(key, 8)
        h6_all = jax.random.normal(ks[0], (N_NODES, D), dtype=jnp.float32)
        edge_index = jax.random.randint(ks[1], (2, N_EDGES), 0, N_NODES, dtype=jnp.int64)
        edge_weight = jax.random.uniform(ks[2], (N_EDGES,), dtype=jnp.float32)
        s = 1.0 / np.sqrt(D)
        W = jax.random.normal(ks[3], (D, D), dtype=jnp.float32) * s
        b = jnp.zeros((D,), dtype=jnp.float32)
        W1 = jax.random.normal(ks[4], (D, D), dtype=jnp.float32) * s
        b1 = jnp.zeros((D,), dtype=jnp.float32)
        W2 = jax.random.normal(ks[5], (D, D), dtype=jnp.float32) * s
        b2 = jnp.zeros((D,), dtype=jnp.float32)
        return {'h6_all': h6_all, 'edge_index': edge_index, 'edge_weight': edge_weight, 'W': W, 'b': b, 'W1': W1, 'b1': b1, 'W2': W2, 'b2': b2}
    _L0_gnn_all = _L0_gnn_setup()
    _L0_gnn_in = {k: v for k, v in _L0_gnn_all.items() if k in ('W', 'b', 'W1', 'b1', 'W2', 'b2')}
    del _L0_gnn_all

    def _L1_gnn_setup():
        import jax, jax.numpy as jnp
        import numpy as np
        N = 3125
        E = 100000
        IN_C = 256
        OUT_C = 256
        key = jax.random.key(seed)
        k1, k2, k3, k4, k5 = jax.random.split(key, 5)
        x = jax.random.normal(k1, (N, IN_C), dtype=jnp.float32)
        edge_index = jax.random.randint(k2, (2, E), 0, N, dtype=jnp.int64)
        limit = np.sqrt(6.0 / (IN_C + OUT_C))
        W = jax.random.uniform(k3, (IN_C, OUT_C), dtype=jnp.float32, minval=-limit, maxval=limit)
        b = jnp.zeros((OUT_C,), dtype=jnp.float32)
        return {'x': x, 'edge_index': edge_index, 'W': W, 'b': b}
    _L1_gnn_all = _L1_gnn_setup()
    _L1_gnn_in = {k: v for k, v in _L1_gnn_all.items() if k in ('W', 'b')}
    del _L1_gnn_all

    def _L2_gnn_setup():
        import jax, jax.numpy as jnp
        import numpy as np
        import math
        L, H, HD, D = (3, 8, 32, 256)
        TN, TE = (4, 3)

        def _layer_norm(x, g, b, eps=1e-05):
            m = jnp.mean(x, axis=-1, keepdims=True)
            v = jnp.var(x, axis=-1, keepdims=True)
            return (x - m) / jnp.sqrt(v + eps) * g + b

        def _typed_transform(xh, W, types):
            out = jnp.zeros_like(xh)
            for t in range(W.shape[0]):
                y = jnp.einsum('mhd,hde->mhe', xh, W[t])
                out = jnp.where((types == t)[:, None, None], y, out)
            return out
        N, E = (625, 10000)
        key = jax.random.key(seed)
        ks = jax.random.split(key, 16)
        inp = {}
        inp['x'] = jax.random.normal(ks[0], (N, D), dtype=jnp.float32)
        inp['edge_index'] = jax.random.randint(ks[1], (2, E), 0, N)
        inp['edge_type'] = jax.random.randint(ks[2], (E,), 0, TE)
        inp['node_type'] = jax.random.randint(ks[3], (N,), 0, TN)
        inp['W_Q'] = jax.random.normal(ks[4], (L, TN, H, HD, HD), dtype=jnp.float32) * 0.02
        inp['W_K'] = jax.random.normal(ks[5], (L, TN, H, HD, HD), dtype=jnp.float32) * 0.02
        inp['W_V'] = jax.random.normal(ks[6], (L, TN, H, HD, HD), dtype=jnp.float32) * 0.02
        inp['W_E'] = jax.random.normal(ks[7], (L, TE, H, HD, HD), dtype=jnp.float32) * 0.02
        inp['mu'] = jnp.ones((L, H, TE), dtype=jnp.float32)
        inp['Wo'] = jax.random.normal(ks[8], (L, D, D), dtype=jnp.float32) * 0.02
        inp['bo'] = jnp.zeros((L, D), dtype=jnp.float32)
        inp['ln1_g'] = jnp.ones((L, D), dtype=jnp.float32)
        inp['ln1_b'] = jnp.zeros((L, D), dtype=jnp.float32)
        inp['ln2_g'] = jnp.ones((L, D), dtype=jnp.float32)
        inp['ln2_b'] = jnp.zeros((L, D), dtype=jnp.float32)
        inp['w1'] = jax.random.normal(ks[9], (L, D, 4 * D), dtype=jnp.float32) * 0.02
        inp['b1'] = jnp.zeros((L, 4 * D), dtype=jnp.float32)
        inp['w2'] = jax.random.normal(ks[10], (L, 4 * D, D), dtype=jnp.float32) * 0.02
        inp['b2'] = jnp.zeros((L, D), dtype=jnp.float32)
        inp['out_g'] = jnp.ones((D,), dtype=jnp.float32)
        inp['out_b'] = jnp.zeros((D,), dtype=jnp.float32)
        return inp
    _L2_gnn_all = _L2_gnn_setup()
    _L2_gnn_in = {k: v for k, v in _L2_gnn_all.items() if k in ('W_Q', 'W_K', 'W_V', 'W_E', 'mu', 'Wo', 'bo', 'ln1_g', 'ln1_b', 'ln2_g', 'ln2_b', 'w1', 'b1', 'w2', 'b2', 'out_g', 'out_b')}
    del _L2_gnn_all

    def _L3_gnn_setup():
        import jax, jax.numpy as jnp
        import numpy as np
        N = 50000
        E = 12500
        IN = 256
        H = 8
        D = 32
        EF = 3
        key = jax.random.key(seed)
        ks = jax.random.split(key, 8)
        x = jax.random.normal(ks[0], (N, IN), dtype=jnp.float32)
        edge_index = jax.random.randint(ks[1], (2, E), 0, N, dtype=jnp.int64)
        edge_attr = jax.random.normal(ks[2], (E, EF), dtype=jnp.float32)
        W = jax.random.normal(ks[3], (H * D, IN), dtype=jnp.float32) * np.float32(np.sqrt(2.0 / (IN + H * D)))
        a_src = jax.random.normal(ks[4], (H, D), dtype=jnp.float32) * np.float32(np.sqrt(2.0 / (H + D)))
        a_dst = jax.random.normal(ks[5], (H, D), dtype=jnp.float32) * np.float32(np.sqrt(2.0 / (H + D)))
        edge_W = jax.random.normal(ks[6], (H * D, EF), dtype=jnp.float32) * np.float32(np.sqrt(2.0 / (EF + H * D)))
        edge_b = jnp.zeros((H * D,), dtype=jnp.float32)
        bias = jnp.zeros((H * D,), dtype=jnp.float32)
        return {'x': x, 'W': W, 'a_src': a_src, 'a_dst': a_dst, 'edge_W': edge_W, 'edge_b': edge_b, 'bias': bias, 'edge_attr': edge_attr, 'edge_index': edge_index}
    _L3_gnn_all = _L3_gnn_setup()
    _L3_gnn_in = {k: v for k, v in _L3_gnn_all.items() if k in ('W', 'a_src', 'a_dst', 'edge_W', 'edge_b', 'bias')}
    del _L3_gnn_all
    return {'x': x, 'src': src, 'dst': dst, 'edge_attr_3': edge_attr_3, 'edge_type_3': edge_type_3, 'edge_weight': edge_weight, 'node_type_4': node_type_4, 'L0_gnn_W': _L0_gnn_in['W'], 'L0_gnn_b': _L0_gnn_in['b'], 'L0_gnn_W1': _L0_gnn_in['W1'], 'L0_gnn_b1': _L0_gnn_in['b1'], 'L0_gnn_W2': _L0_gnn_in['W2'], 'L0_gnn_b2': _L0_gnn_in['b2'], 'L1_gnn_W': _L1_gnn_in['W'], 'L1_gnn_b': _L1_gnn_in['b'], 'L2_gnn_W_Q': _L2_gnn_in['W_Q'], 'L2_gnn_W_K': _L2_gnn_in['W_K'], 'L2_gnn_W_V': _L2_gnn_in['W_V'], 'L2_gnn_W_E': _L2_gnn_in['W_E'], 'L2_gnn_mu': _L2_gnn_in['mu'], 'L2_gnn_Wo': _L2_gnn_in['Wo'], 'L2_gnn_bo': _L2_gnn_in['bo'], 'L2_gnn_ln1_g': _L2_gnn_in['ln1_g'], 'L2_gnn_ln1_b': _L2_gnn_in['ln1_b'], 'L2_gnn_ln2_g': _L2_gnn_in['ln2_g'], 'L2_gnn_ln2_b': _L2_gnn_in['ln2_b'], 'L2_gnn_w1': _L2_gnn_in['w1'], 'L2_gnn_b1': _L2_gnn_in['b1'], 'L2_gnn_w2': _L2_gnn_in['w2'], 'L2_gnn_b2': _L2_gnn_in['b2'], 'L2_gnn_out_g': _L2_gnn_in['out_g'], 'L2_gnn_out_b': _L2_gnn_in['out_b'], 'L3_gnn_W': _L3_gnn_in['W'], 'L3_gnn_a_src': _L3_gnn_in['a_src'], 'L3_gnn_a_dst': _L3_gnn_in['a_dst'], 'L3_gnn_edge_W': _L3_gnn_in['edge_W'], 'L3_gnn_edge_b': _L3_gnn_in['edge_b'], 'L3_gnn_bias': _L3_gnn_in['bias']}

def reference(x, src, dst, edge_attr_3, edge_type_3, edge_weight, node_type_4, L0_gnn_W, L0_gnn_b, L0_gnn_W1, L0_gnn_b1, L0_gnn_W2, L0_gnn_b2, L1_gnn_W, L1_gnn_b, L2_gnn_W_Q, L2_gnn_W_K, L2_gnn_W_V, L2_gnn_W_E, L2_gnn_mu, L2_gnn_Wo, L2_gnn_bo, L2_gnn_ln1_g, L2_gnn_ln1_b, L2_gnn_ln2_g, L2_gnn_ln2_b, L2_gnn_w1, L2_gnn_b1, L2_gnn_w2, L2_gnn_b2, L2_gnn_out_g, L2_gnn_out_b, L3_gnn_W, L3_gnn_a_src, L3_gnn_a_dst, L3_gnn_edge_W, L3_gnn_edge_b, L3_gnn_bias):
    import jax
    import jax.numpy as jnp

    def _L0_gnn_ref(h6_all, edge_index, edge_weight, W, b, W1, b1, W2, b2):
        import jax, jax.numpy as jnp
        import numpy as np
        N_NODES = 3125
        N_EDGES = 50000
        D = 256
        'GCNConv(256->256, weighted, self-loops, symmetric norm) + 2-layer MLP head.'
        N = h6_all.shape[0]
        row, col = (edge_index[0], edge_index[1])
        sl = jnp.arange(N, dtype=edge_index.dtype)
        row_sl = jnp.concatenate([row, sl])
        col_sl = jnp.concatenate([col, sl])
        ew_sl = jnp.concatenate([edge_weight, jnp.ones((N,), dtype=edge_weight.dtype)])
        deg = jax.ops.segment_sum(ew_sl, row_sl, num_segments=N)
        dinv = jnp.where(deg > 0, jax.lax.rsqrt(deg), 0.0)
        norm = dinv[row_sl] * ew_sl * dinv[col_sl]
        xw = h6_all @ W
        msgs = xw[col_sl] * norm[:, None]
        h7 = jax.ops.segment_sum(msgs, row_sl, num_segments=N) + b
        h = jax.nn.relu(h7 @ W1 + b1)
        out = h @ W2 + b2
        return out

    def _L1_gnn_ref(x, edge_index, W, b):
        import jax, jax.numpy as jnp
        import numpy as np
        N = 3125
        E = 100000
        IN_C = 256
        OUT_C = 256
        n = x.shape[0]
        h = x @ W
        loop = jnp.arange(n, dtype=edge_index.dtype)
        row = jnp.concatenate([edge_index[0], loop])
        col = jnp.concatenate([edge_index[1], loop])
        ones = jnp.ones(row.shape[0], dtype=h.dtype)
        deg = jax.ops.segment_sum(ones, col, num_segments=n)
        dinv = jnp.where(deg > 0, jax.lax.rsqrt(deg), 0.0)
        norm = dinv[row] * dinv[col]
        msg = h[row] * norm[:, None]
        out = jax.ops.segment_sum(msg, col, num_segments=n)
        out = out + b
        return jax.nn.relu(out)

    def _L2_gnn_ref(x, edge_index, edge_type, node_type, W_Q, W_K, W_V, W_E, mu, Wo, bo, ln1_g, ln1_b, ln2_g, ln2_b, w1, b1, w2, b2, out_g, out_b):
        import jax, jax.numpy as jnp
        import numpy as np
        import math
        L, H, HD, D = (3, 8, 32, 256)
        TN, TE = (4, 3)

        def _layer_norm(x, g, b, eps=1e-05):
            m = jnp.mean(x, axis=-1, keepdims=True)
            v = jnp.var(x, axis=-1, keepdims=True)
            return (x - m) / jnp.sqrt(v + eps) * g + b

        def _typed_transform(xh, W, types):
            out = jnp.zeros_like(xh)
            for t in range(W.shape[0]):
                y = jnp.einsum('mhd,hde->mhe', xh, W[t])
                out = jnp.where((types == t)[:, None, None], y, out)
            return out
        N = x.shape[0]
        src, dst = (edge_index[0], edge_index[1])
        scale = math.sqrt(HD)
        for l in range(L):
            xh = x.reshape(N, H, HD)
            Q = _typed_transform(xh, W_Q[l], node_type)
            K = _typed_transform(xh, W_K[l], node_type)
            V = _typed_transform(xh, W_V[l], node_type)
            q_dst = Q[dst]
            kt = _typed_transform(K[src], W_E[l], edge_type)
            scores = jnp.sum(q_dst * kt, axis=-1) / scale
            scores = scores * mu[l].T[edge_type]
            m = jax.ops.segment_max(scores, dst, num_segments=N)
            m = jnp.maximum(m, -1000000000.0)
            e = jnp.exp(scores - m[dst])
            s = jax.ops.segment_sum(e, dst, num_segments=N)
            w = e / (s[dst] + 1e-10)
            agg = jax.ops.segment_sum(V[src] * w[..., None], dst, num_segments=N)
            attn = agg.reshape(N, D) @ Wo[l] + bo[l]
            x = _layer_norm(x + attn, ln1_g[l], ln1_b[l])
            h = jax.nn.gelu(x @ w1[l] + b1[l], approximate=False) @ w2[l] + b2[l]
            x = _layer_norm(x + h, ln2_g[l], ln2_b[l])
        return _layer_norm(x, out_g, out_b)

    def _L3_gnn_ref(x, W, a_src, a_dst, edge_W, edge_b, bias, edge_attr, edge_index):
        import jax, jax.numpy as jnp
        import numpy as np
        N = 50000
        E = 12500
        IN = 256
        H = 8
        D = 32
        EF = 3
        n = x.shape[0]
        h = (x @ W.T).reshape(n, H, D)
        src, dst = (edge_index[0], edge_index[1])
        h_src = h[src]
        h_dst = h[dst]
        alpha = jnp.einsum('ehd,hd->eh', h_src, a_src) + jnp.einsum('ehd,hd->eh', h_dst, a_dst)
        enc = jax.nn.relu(edge_attr @ edge_W.T + edge_b).reshape(-1, H, D)
        alpha = alpha + jnp.sum(enc * h_dst, axis=-1)
        alpha = jnp.where(alpha >= 0, alpha, 0.2 * alpha)
        amax = jax.ops.segment_max(alpha, dst, num_segments=n)
        ex = jnp.exp(alpha - amax[dst])
        denom = jax.ops.segment_sum(ex, dst, num_segments=n)
        attn = ex / jnp.maximum(denom[dst], 1e-10)
        out = jax.ops.segment_sum(h_src * attn[..., None], dst, num_segments=n)
        return out.reshape(n, H * D) + bias
    edge_index = jnp.stack([src, dst])
    h = jnp.maximum(_layernorm(x, axis=-1), 0.0)
    x = x + _L0_gnn_ref(h, edge_index, edge_weight, L0_gnn_W, L0_gnn_b, L0_gnn_W1, L0_gnn_b1, L0_gnn_W2, L0_gnn_b2)
    h = jnp.maximum(_layernorm(x, axis=-1), 0.0)
    x = x + _L1_gnn_ref(h, edge_index, L1_gnn_W, L1_gnn_b)
    h = jnp.maximum(_layernorm(x, axis=-1), 0.0)
    x = x + _L2_gnn_ref(h, edge_index, edge_type_3, node_type_4, L2_gnn_W_Q, L2_gnn_W_K, L2_gnn_W_V, L2_gnn_W_E, L2_gnn_mu, L2_gnn_Wo, L2_gnn_bo, L2_gnn_ln1_g, L2_gnn_ln1_b, L2_gnn_ln2_g, L2_gnn_ln2_b, L2_gnn_w1, L2_gnn_b1, L2_gnn_w2, L2_gnn_b2, L2_gnn_out_g, L2_gnn_out_b)
    h = jnp.maximum(_layernorm(x, axis=-1), 0.0)
    x = x + _L3_gnn_ref(h, L3_gnn_W, L3_gnn_a_src, L3_gnn_a_dst, L3_gnn_edge_W, L3_gnn_edge_b, L3_gnn_bias, edge_attr_3, edge_index)
    return x

_drawn_inputs = setup_inputs


def setup_inputs(seed=0):
    import zlib

    import numpy as np

    out = dict(_drawn_inputs(seed))
    spreads = {'L0_gnn_b': (0.0, 0.1),
     'L0_gnn_b1': (0.0, 0.1),
     'L0_gnn_b2': (0.0, 0.1),
     'L1_gnn_b': (0.0, 0.1),
     'L2_gnn_mu': (1.0, 0.6),
     'L2_gnn_bo': (0.0, 0.1),
     'L2_gnn_ln1_g': (1.0, 0.2),
     'L2_gnn_ln1_b': (0.0, 0.1),
     'L2_gnn_ln2_g': (1.0, 0.2),
     'L2_gnn_ln2_b': (0.0, 0.1),
     'L2_gnn_b1': (0.0, 0.275),
     'L2_gnn_b2': (0.0, 0.1),
     'L2_gnn_out_g': (1.0, 0.2),
     'L2_gnn_out_b': (0.0, 0.1),
     'L3_gnn_edge_b': (0.0, 1.468),
     'L3_gnn_bias': (0.0, 0.1)}
    factors = {'L2_gnn_W_Q': 8.0,
     'L2_gnn_W_K': 8.0,
     'L2_gnn_W_V': 4.709,
     'L2_gnn_W_E': 8.0,
     'L2_gnn_Wo': 4.59,
     'L3_gnn_a_dst': 8.597}
    for name, (base, spread) in spreads.items():
        noise = np.random.default_rng([zlib.crc32(name.encode()), seed]).standard_normal(out[name].shape)
        drawn = base * np.exp(spread * noise) if base else spread * noise
        out[name] = jnp.asarray(drawn.astype(out[name].dtype))
    for name, factor in factors.items():
        out[name] = (out[name] * factor).astype(out[name].dtype)
    return out
```

```python
import concourse.bass as bass
from concourse import mybir
from contextlib import ExitStack

F32 = mybir.dt.float32
I32 = mybir.dt.int32
ALU = mybir.AluOpType
ACT = mybir.ActivationFunctionType
AX = mybir.AxisListType

P = 128
N = 3125
NB = 25
NP = NB * P
D = 256
H = 8
HD = D // H
HC = HD + 1
VC = H * HC
E = 53125
T = 418
ER = P * T
EF = 8
SF = 4
PAIR = 2 * P
NPR = (E + NB * (PAIR - 1)) // PAIR
GP = 4
GT = 2 * GP
NG = NPR // GP
NT = 2 * NPR
U = 5
BIG = float(1 << 20)
FAR = 1.0e30
SRC, DST = 0, 1
assert NPR % (2 * GP) == 0 and NB % U == 0 and T % 22 == 0


def wait(eng, sem, value):
    eng.wait_ge(sem, value)
    if not isinstance(value, int):
        eng.nop(nofuse=True)


def at(tensor, index):
    if isinstance(index, int):
        return tensor[:, index, :]
    return tensor[:, bass.ds(index, 1), :].rearrange("p a b -> p (a b)")


def spread(ap, axis, count):
    shape = list(ap.shape)
    shape.insert(axis, count)
    return ap.unsqueeze(axis).broadcast_to(shape)


class Stage:

    def __init__(self, nc, name):
        self.nc, self.name, self.stack, self.sems = nc, name, ExitStack(), []

    def __enter__(self):
        return self

    def __exit__(self, *args):
        self.stack.close()
        numbers = sorted(x.num for x in self.sems)
        while numbers:
            end = next((k for k in range(1, len(numbers)) if numbers[k] != numbers[0] + k), len(numbers))
            self.nc.gpsimd.dma_reset(range(numbers[0], numbers[0] + end))
            self.nc.gpsimd.sem_clear(range(numbers[0], numbers[0] + end))
            numbers = numbers[end:]

    def sb(self, name, shape, dt=F32):
        return self.stack.enter_context(self.nc.sbuf_tensor(f"{self.name}_{name}", shape, dt))

    def ps(self, name, shape, dt=F32):
        return self.stack.enter_context(self.nc.psum_tensor(f"{self.name}_{name}", shape, dt))

    def sem(self, name):
        self.sems.append(self.stack.enter_context(self.nc.semaphore(f"{self.name}_{name}")))
        return self.sems[-1]

    def block(self):
        return self.stack.enter_context(self.nc.Block())


def constants(nc, c):
    with Stage(nc, "const") as st:
        filled, counted, made = st.sem("filled"), st.sem("counted"), st.sem("made")
        count_i, starts_i, turns_i = st.sb("count_i", [P, P], I32), st.sb("starts_i", [P, NB + 1], I32), st.sb(
            "turns_i", [P, NPR], I32)
        edge_i = st.sb("edge_i", [P, T], I32)
        block = st.block()

        @block.gpsimd
        def _(pool):
            for t in (c.ident, c.down, c.up, c.zeros):
                pool.memset(t[:, :], 0.0).then_inc(filled, 1)
            for t in (c.ones, c.upper):
                pool.memset(t[:, :], 1.0).then_inc(filled, 1)
            pool.iota(count_i[:, :], pattern=[[1, P]], base=0, channel_multiplier=0)
            pool.iota(starts_i[:, :], pattern=[[P, NB + 1]], base=0, channel_multiplier=0)
            pool.iota(turns_i[:, :], pattern=[[1, NPR]], base=0, channel_multiplier=0)
            pool.iota(edge_i[:, :], pattern=[[1, T]], base=0, channel_multiplier=T).then_inc(counted, 1)
            pool.wait_ge(filled, 6)
            for t, base in ((c.ident, 0), (c.down, -1), (c.up, 1)):
                pool.affine_select(out=t[:, :], in_=t[:, :], compare_op=ALU.not_equal, fill=1.0, base=base,
                                   pattern=[[-1, P]], channel_multiplier=1)
            pool.affine_select(out=c.upper[:, :], in_=c.upper[:, :], compare_op=ALU.is_gt, fill=0.0, base=0,
                               pattern=[[1, P]], channel_multiplier=-1)

        @block.vector
        def _(dve):
            dve.wait_ge(counted, 1)
            dve.tensor_copy(c.count[:, :], count_i[:, :])
            dve.tensor_copy(c.starts[:, :], starts_i[:, :])
            dve.tensor_copy(c.turns[:, :], turns_i[:, :])
            dve.tensor_copy(c.edge[:, :], edge_i[:, :]).then_inc(made, 1)


def load_edges(nc, c, a):
    with Stage(nc, "edges") as st:
        ints = [st.sb(f"int{k}", [P, T], I32) for k in range(3)]
        weight, attr = st.sb("weight", [P, T]), st.sb("attr", [P, T, 3])
        junk = st.sb("junk", [P, T])
        less = st.sb("less", [P, 2, NB + 1])
        total = st.ps("total", [P, 2, NB + 1])
        cleared, landed, packed, counted, summed, stored = (
            st.sem(x) for x in ("cleared", "landed", "packed", "counted", "summed", "stored"))
        block = st.block()
        whole = E // T
        cut = whole // 16 * 16

        @block.sync
        def _(sp):
            sp.wait_ge(cleared, 1)
            for to, source, w in ((ints[0], a["src"], 1), (ints[1], a["dst"], 1), (ints[2], a["edge_type_3"], 1),
                                  (weight, a["edge_weight"], 1), (attr, a["edge_attr_3"], 3)):
                flat = source if w == 1 else source.rearrange("e k -> (e k)")
                to = to[:, :] if w == 1 else to[:, :, :].rearrange("p t k -> p (t k)")
                rows = flat[0:whole * T * w].rearrange("(p t) -> p t", t=T * w)
                rest = flat[whole * T * w:E * w].rearrange("(p t) -> p t", p=1)
                sp.dma_start(to[0:cut, :], rows[0:cut, :]).then_inc(landed, 16)
                sp.dma_start(to[cut:whole, :], rows[cut:whole, :]).then_inc(landed, 16)
                sp.dma_start(to[whole:whole + 1, 0:(E - whole * T) * w], rest).then_inc(landed, 16)
            sp.wait_ge(packed, 1)
            sp.dma_start(c.edge_rows.rearrange("(p t) f -> p (t f)", t=T),
                         c.pack[:, :, :].rearrange("p t f -> p (t f)")).then_inc(stored, 16)
            sp.wait_ge(stored, 16)

        @block.vector
        def _(dve):
            dve.memset(ints[0][:, :], 1 << 20)
            dve.memset(ints[1][:, :], 1 << 20)
            dve.memset(ints[2][:, :], 0)
            dve.memset(weight[:, :], 0.0)
            dve.memset(c.pack[:, :, 7], 1.0)
            dve.memset(attr[:, :, :], 0.0).then_inc(cleared, 1)
            dve.wait_ge(landed, 15 * 16)
            for k in range(3):
                dve.tensor_copy(c.pack[:, :, k], ints[k][:, :])
            dve.tensor_copy(c.pack[:, :, 3], weight[:, :])
            dve.tensor_copy(c.pack[:, :, 4:7], attr[:, :, :]).then_inc(packed, 1)
            dve.wait_ge(packed, 1)
            for b in range(NB + 1):
                for o in (SRC, DST):
                    n = 2 * b + o
                    if n:
                        dve.wait_ge(counted, n)
                    dve.tensor_scalar(junk[:, :], c.pack[:, :, o], float(P * b), 0.0, ALU.is_lt, ALU.add,
                                      accum_out=less[:, o, b:b + 1]).then_inc(counted, 1)
            dve.wait_ge(summed, 1)
            dve.tensor_copy(c.first[:, :, :], total[:, :, :])

        @block.tensor
        def _(pe):
            pe.wait_ge(counted, 2 * (NB + 1))
            pe.matmul(total[:, :, :].rearrange("p o b -> p (o b)"), c.ones[:, :],
                      less[:, :, :].rearrange("p o b -> p (o b)"), start=True, stop=True).then_inc(summed, 1)


def pair_tables(nc, c):
    with Stage(nc, "pairs") as st:
        size, size_i = st.sb("size", [P, 2, NB]), st.sb("size_i", [P, 2, NB], I32)
        before, offset, step = st.sb("before", [P, 2, NB + 1]), st.sb("offset", [P, 2, NB + 1]), st.sb(
            "step", [P, 2, NB + 1])
        reached, stepped = st.sb("reached", [P, NPR, NB + 1]), st.sb("stepped", [P, NPR, NB + 1])
        nothing, start = st.sb("nothing", [P, NB]), st.sb("start", [P, 2, NPR])
        done = st.sem("done")
        block = st.block()

        @block.vector
        def _(dve):
            count = [0]

            def then(instruction):
                count[0] += 1
                instruction.then_inc(done, 1)
                dve.wait_ge(done, count[0])

            dve.memset(nothing[:, :], 0.0)
            dve.memset(before[:, :, 0], 0.0)
            then(dve.tensor_tensor(size[:, :, :], c.first[:, :, 1:], c.first[:, :, :NB], ALU.subtract))
            then(dve.tensor_scalar(size_i[:, :, :], size[:, :, :], float(PAIR - 1), None, ALU.add))
            then(dve.tensor_scalar(size_i[:, :, :], size_i[:, :, :], 8, None, ALU.arith_shift_right))
            then(dve.tensor_copy(size[:, :, :], size_i[:, :, :]))
            for o in (SRC, DST):
                then(dve.tensor_tensor_scan(before[:, o, 1:], size[:, o, :], nothing[:, :], 0.0, ALU.add, ALU.add))
            then(dve.scalar_tensor_tensor(offset[:, :, :], before[:, :, :], -float(PAIR), c.first[:, :, :], ALU.mult,
                                          ALU.add))
            dve.tensor_copy(step[:, :, 0], offset[:, :, 0])
            then(dve.tensor_tensor(step[:, :, 1:], offset[:, :, 1:], offset[:, :, :NB], ALU.subtract))
            for o in (SRC, DST):
                then(dve.tensor_tensor(reached[:, :, :], spread(before[:, o, :], 1, NPR),
                                       spread(c.turns[:, :], 2, NB + 1), ALU.is_le))
                then(dve.tensor_reduce(c.block[:, o, :], reached[:, :, 1:], AX.X, ALU.add))
                then(dve.tensor_scalar(c.block[:, o, :], c.block[:, o, :], float(NB - 1), None, ALU.min))
                then(dve.tensor_tensor(stepped[:, :, :], reached[:, :, :], spread(step[:, o, :], 1, NPR), ALU.mult))
                then(dve.tensor_reduce(start[:, o, :], stepped[:, :, :], AX.X, ALU.add))
                then(dve.scalar_tensor_tensor(start[:, o, :], c.turns[:, :], float(PAIR), start[:, o, :], ALU.mult,
                                              ALU.add))
                then(dve.tensor_scalar(start[:, o, :], start[:, o, :], float(E), None, ALU.min))
            dve.tensor_copy(c.start_i[:, :, :], start[:, :, :])
            dve.tensor_copy(c.block_i[:, :, :], c.block[:, :, :])


def rank_sources(nc, c):
    with Stage(nc, "rank") as st:
        key, key_i = st.sb("key", [P, T]), st.sb("key_i", [P, T], I32)
        one, many, part = st.sb("one", [P, T]), st.sb("many", [P, T]), st.sb("part", [P, T])
        nothing, place = st.sb("nothing", [P, T]), st.sb("place", [P, T])
        held, base = st.sb("held", [P, NB]), st.sb("base", [P, NB])
        above = st.ps("above", [P, NB])
        done, held_ready, above_ready = st.sem("done"), st.sem("held_ready"), st.sem("above_ready")
        block = st.block()

        @block.vector
        def _(dve):
            count = [0]

            def then(instruction):
                count[0] += 1
                instruction.then_inc(done, 1)
                dve.wait_ge(done, count[0])

            dve.memset(nothing[:, :], 0.0)
            then(dve.tensor_copy(key_i[:, :], c.pack[:, :, SRC]))
            then(dve.tensor_scalar(key_i[:, :], key_i[:, :], 7, None, ALU.arith_shift_right))
            then(dve.tensor_copy(key[:, :], key_i[:, :]))
            then(dve.scalar_tensor_tensor(place[:, :], c.edge[:, :], float(E), c.edge[:, :], ALU.is_ge, ALU.mult))
            for b in range(NB):
                then(dve.tensor_scalar(one[:, :], key[:, :], float(b), None, ALU.is_equal))
                then(dve.tensor_tensor_scan(many[:, :], one[:, :], nothing[:, :], 0.0, ALU.add, ALU.add))
                dve.tensor_copy(held[:, b:b + 1], many[:, T - 1:T])
                then(dve.tensor_tensor(part[:, :], one[:, :], many[:, :], ALU.mult))
                then(dve.tensor_tensor(place[:, :], place[:, :], part[:, :], ALU.add))
            dve.drain().then_inc(held_ready, 1)
            dve.wait_ge(above_ready, 1)
            then(dve.scalar_tensor_tensor(base[:, :], above[:, :], -1.0, c.first[:, SRC, :NB], ALU.add, ALU.add))
            for b in range(NB):
                then(dve.tensor_scalar(part[:, :], key[:, :], float(b), base[:, b:b + 1], ALU.is_equal, ALU.mult))
                then(dve.tensor_tensor(place[:, :], place[:, :], part[:, :], ALU.add))
            dve.tensor_copy(c.place[:, :], place[:, :])
            dve.tensor_copy(c.by_source[:, :, 0], c.pack[:, :, 1])
            dve.tensor_copy(c.by_source[:, :, 1], c.pack[:, :, 0])
            dve.tensor_copy(c.by_source[:, :, 2], c.pack[:, :, 3])
            dve.tensor_copy(c.by_source[:, :, 3], c.pack[:, :, 7])

        @block.tensor
        def _(pe):
            pe.wait_ge(held_ready, 1)
            pe.matmul(above[:, :], c.upper[:, :], held[:, :], start=True, stop=True).then_inc(above_ready, 1)


def scatter_sources(nc, c):
    B = T // 22
    with Stage(nc, "scatter") as st:
        place = [st.sb(f"place{h}", [P, B], I32) for h in range(2)]
        rows = [st.sb(f"rows{h}", [P, B, SF]) for h in range(2)]
        high_i, high, low = st.sb("high_i", [P, 2, T], I32), st.sb("high", [P, 2, T]), st.sb("low", [P, 2, T])
        lows, highs = st.sb("lows", [P, 2, 2, P]), st.sb("highs", [P, 2, 2, NB])
        sums = [st.ps(f"sums{o}", [P, NB]) for o in range(2)]
        degree, seen = st.sb("degree", [P, 2, NB]), st.sb("seen", [P, 2, NB])
        copied = st.sem("copied")
        stored = [st.sem(f"stored{h}") for h in range(2)]
        split, hot, used, summed = st.sem("split"), st.sem("hot"), st.sem("used"), st.sem("summed")
        safe, rooted = st.sem("safe"), st.sem("rooted")
        block = st.block()

        @block.gpsimd
        def _(pool):
            def scatter(i, h):
                col = (i * 2 + h) * B
                if not isinstance(i, int):
                    wait(pool, stored[h], i * (16 * B))
                pool.tensor_copy(place[h][:, :], c.place[:, bass.ds(col, B)])
                pool.tensor_copy(rows[h][:, :, :], c.by_source[:, bass.ds(col, B), :]).then_inc(copied, 1)
                wait(pool, copied, i * 2 + h + 1)
                for k in range(B):
                    pool.indirect_dma_start(c.source_rows, bass.IndirectOffsetOnAxis(ap=place[h][:, k:k + 1], axis=0),
                                            rows[h][:, k, :], None).then_inc(stored[h], 16)

            scatter(0, 0)
            scatter(0, 1)
            with pool.Fori(1, T // (2 * B)) as i:
                scatter(i, 0)
                scatter(i, 1)
            for h in range(2):
                pool.wait_ge(stored[h], 16 * B * (T // (2 * B)))

        @block.vector
        def _(dve):
            for o in (SRC, DST):
                dve.tensor_copy(high_i[:, o, :], c.pack[:, :, o]).then_inc(split, 1)
            dve.wait_ge(split, 2)
            dve.tensor_scalar(high_i[:, :, :], high_i[:, :, :], 7, None, ALU.arith_shift_right).then_inc(split, 1)
            dve.wait_ge(split, 3)
            dve.tensor_copy(high[:, :, :], high_i[:, :, :]).then_inc(split, 1)
            dve.wait_ge(split, 4)
            for o in (SRC, DST):
                dve.scalar_tensor_tensor(low[:, o, :], high[:, o, :], -float(P), c.pack[:, :, o], ALU.mult,
                                         ALU.add).then_inc(split, 1)
            dve.wait_ge(split, 6)
            with dve.Fori(0, T // 2) as i:
                for s in range(2):
                    t = i * 2 + s
                    wait(dve, used, t + 1)
                    for o in (SRC, DST):
                        dve.tensor_scalar(lows[:, s, o, :], c.count[:, :], low[:, o, bass.ds(t, 1)], None, ALU.is_equal)
                    dve.tensor_scalar(highs[:, s, SRC, :], c.count[:, :NB], high[:, SRC, bass.ds(t, 1)],
                                      c.pack[:, bass.ds(t, 1), 3], ALU.is_equal, ALU.mult)
                    dve.tensor_scalar(highs[:, s, DST, :], c.count[:, :NB], high[:, DST, bass.ds(t, 1)], None,
                                      ALU.is_equal).then_inc(hot, 1)
            dve.wait_ge(summed, 1)
            for o in (SRC, DST):
                dve.tensor_scalar(degree[:, o, :], sums[o][:, :], 1.0, None, ALU.add).then_inc(safe, 1)
            dve.wait_ge(safe, 2)
            dve.tensor_scalar(seen[:, :, :], degree[:, :, :], 0.0, None, ALU.is_gt)
            dve.tensor_scalar(degree[:, :, :], degree[:, :, :], 1e-30, None, ALU.max).then_inc(safe, 1)
            dve.wait_ge(safe, 3)
            dve.reciprocal(degree[:, :, :], degree[:, :, :]).then_inc(safe, 1)
            dve.wait_ge(rooted, 1)
            dve.tensor_tensor(c.dinv[:, :, :], c.dinv[:, :, :], seen[:, :, :], ALU.mult)

        @block.scalar
        def _(act):
            act.wait_ge(safe, 4)
            act.activation(c.dinv[:, :, :], degree[:, :, :], ACT.Sqrt).then_inc(rooted, 1)

        @block.tensor
        def _(pe):
            for o in (SRC, DST):
                pe.matmul(sums[o][:, :], c.zeros[:, :], c.zeros[:, :NB], start=True, stop=False).then_inc(used, 1)
            with pe.Fori(0, T // 2) as i:
                for s in range(2):
                    wait(pe, hot, i * 2 + s + 1)
                    pe.matmul(sums[SRC][:, :], lows[:, s, SRC, :], highs[:, s, SRC, :], start=False, stop=False)
                    pe.matmul(sums[DST][:, :], lows[:, s, DST, :], highs[:, s, DST, :], start=False,
                              stop=False).then_inc(used, 1)
            for o in (SRC, DST):
                last = pe.matmul(sums[o][:, :], c.zeros[:, :], c.zeros[:, :NB], start=False, stop=True)
            last.then_inc(summed, 1)


def load_pairs(nc, c):
    with Stage(nc, "meta") as st:
        rows = st.sb("rows", [P, NT, SF])
        landed = [st.sem(f"landed{o}") for o in range(2)]
        done, shifted = st.sem("done"), st.sem("shifted")
        key = [st.sb(f"key{o}", [P, NT]) for o in range(2)]
        index, edge = st.sb("index", [P, NT]), st.sb("edge", [P, NT])
        other = [st.ps(f"other{k}", [P, NT]) for k in range(2)]
        block = st.block()

        def fetch(eng, o, source, to):
            with eng.Fori(0, NPR // 8) as i:
                for k in range(8):
                    j = i * 8 + k
                    first = eng.value_load(c.start_i[0:1, o, bass.ds(j, 1)], min_val=0, max_val=E)
                    eng.dma_start(to[:, bass.ds(j * 2, 2), :].rearrange("p k f -> p (k f)"),
                                  source[bass.ds(first, PAIR), :].rearrange("(p k) f -> p (k f)", k=2)
                                  ).then_inc(landed[o], 16)

        @block.sync
        def _(sp):
            fetch(sp, DST, c.edge_rows, c.meta)

        @block.scalar
        def _(act):
            fetch(act, SRC, c.source_rows, rows)

        @block.vector
        def _(dve):
            count = [0]

            def then(instruction):
                count[0] += 1
                instruction.then_inc(done, 1)
                dve.wait_ge(done, count[0])

            for o, source in ((SRC, rows), (DST, c.meta)):
                dve.wait_ge(landed[o], 16 * NPR)
                then(dve.tensor_scalar(key[o][:, :], source[:, :, 1], 1.0, None, ALU.add))
                then(dve.scalar_tensor_tensor(c.local[:, o, :].rearrange("p (j k) -> p j k", k=2),
                                              spread(c.block[:, o, :], 2, 2), -float(P),
                                              source[:, :, 1].rearrange("p (j k) -> p j k", k=2), ALU.mult, ALU.add))
                then(dve.tensor_scalar(index[:, :], source[:, :, 0], float(NP - 1), None, ALU.min))
                then(dve.tensor_copy(c.index[:, o, :], index[:, :]))
            dve.tensor_copy(c.weight[:, :], rows[:, :, 2])
            dve.scalar_tensor_tensor(c.typed_index[:, :], c.meta[:, :, 2], float(NP), index[:, :], ALU.mult, ALU.add)
            dve.wait_ge(shifted, 1)
            then(dve.tensor_tensor(edge[:, :], other[0][:, :], key[DST][:, :], ALU.not_equal))
            then(dve.scalar_tensor_tensor(c.last[:, :], c.local[:, DST, :], 1.0, edge[:, :], ALU.add, ALU.mult))
            then(dve.tensor_scalar(c.last[:, :], c.last[:, :], -1.0, None, ALU.add))
            then(dve.tensor_tensor(edge[:, :], other[1][:, :], key[DST][:, :], ALU.not_equal))
            dve.tensor_scalar(c.fresh[:, :], edge[:, :], -FAR, None, ALU.mult)

        @block.tensor
        def _(pe):
            pe.wait_ge(done, 5)
            pe.matmul(other[0][:, :], c.down[:, :], key[DST][:, :], start=True, stop=True)
            pe.matmul(other[1][:, :], c.up[:, :], key[DST][:, :], start=True, stop=True).then_inc(shifted, 1)


def normalize(nc, c, name, source, target, relu=False, gain=None, bias=None, add_to=None):
    with Stage(nc, name) as st:
        stats = st.sb("stats", [P, NB, 6])
        mean, var, gap = st.sb("mean", [P, NB]), st.sb("var", [P, NB]), st.sb("gap", [P, NB])
        scaled = [st.sb(f"scaled{s}", [P, D]) for s in range(U)]
        done, safe, rooted, counted = st.sem("done"), st.sem("safe"), st.sem("rooted"), st.sem("counted")
        centered, gained, biased, ended = (st.sem(x) for x in ("centered", "gained", "biased", "ended"))
        block = st.block()

        @block.vector
        def _(dve):
            count = [0]

            def then(instruction):
                count[0] += 1
                instruction.then_inc(done, 1)
                dve.wait_ge(done, count[0])

            with dve.Fori(0, NB // U) as i:
                for s in range(U):
                    last = dve.bn_stats(at(stats, i * U + s), at(source, i * U + s))
            dve.drain().then_inc(counted, 1)
            dve.wait_ge(counted, 1)
            then(dve.tensor_tensor(mean[:, :], stats[:, :, 1], stats[:, :, 4], ALU.add))
            then(dve.tensor_tensor(gap[:, :], stats[:, :, 1], stats[:, :, 4], ALU.subtract))
            then(dve.tensor_scalar(mean[:, :], mean[:, :], 0.5, None, ALU.mult))
            then(dve.tensor_tensor(gap[:, :], gap[:, :], gap[:, :], ALU.mult))
            then(dve.tensor_tensor(var[:, :], stats[:, :, 2], stats[:, :, 5], ALU.add))
            then(dve.tensor_scalar(var[:, :], var[:, :], 1.0 / D, 1e-5, ALU.mult, ALU.add))
            then(dve.scalar_tensor_tensor(var[:, :], gap[:, :], 0.25, var[:, :], ALU.mult, ALU.add))
            dve.reciprocal(var[:, :], var[:, :]).then_inc(safe, 1)
            dve.wait_ge(rooted, 1)
            dve.sem_inc(ended, U)
            with dve.Fori(0, NB // U) as i:
                own = gain is not None or add_to is not None
                if own:
                    wait(dve, ended, i * U + U)
                for s in range(U):
                    t = i * U + s
                    dve.tensor_scalar(scaled[s][:, :] if own else at(target, t), at(source, t),
                                      mean[:, bass.ds(t, 1)], gap[:, bass.ds(t, 1)], ALU.subtract,
                                      ALU.mult).then_inc(centered, 1)
                wait(dve, centered, i * U + U)
                if relu:
                    for s in range(U):
                        dve.tensor_scalar(at(target, i * U + s), at(target, i * U + s), 0.0, None, ALU.max)
                if gain is not None:
                    for s in range(U):
                        dve.tensor_tensor(scaled[s][:, :], scaled[s][:, :], gain, ALU.mult).then_inc(gained, 1)
                    wait(dve, gained, i * U + U)
                    for s in range(U):
                        to = at(target, i * U + s) if add_to is None else scaled[s][:, :]
                        dve.tensor_tensor(to, scaled[s][:, :], bias, ALU.add).then_inc(
                            ended if add_to is None else biased, 1)
                if add_to is not None:
                    wait(dve, biased, i * U + U)
                    for s in range(U):
                        dve.tensor_tensor(at(add_to, i * U + s), at(add_to, i * U + s), scaled[s][:, :],
                                          ALU.add).then_inc(ended, 1)

        @block.scalar
        def _(act):
            act.wait_ge(safe, 1)
            act.activation(gap[:, :], var[:, :], ACT.Sqrt).then_inc(rooted, 1)


def each_block(eng, body):
    with eng.Fori(0, NB // 2) as i:
        for s in range(2):
            body(i * 2 + s, s)
    body(NB - 1, (NB - 1) % 2)


def copy_blocks(block, source, here, here_ready, flipped):
    @block.gpsimd
    def _(pool):
        def copy(t, s):
            if not (isinstance(t, int) and t < 2):
                wait(pool, flipped, t - 1)
            pool.tensor_copy(here[s][:, :], at(source, t)).then_inc(here_ready, 1)

        copy(0, 0)
        copy(1, 1)
        with pool.Fori(1, NB // 2) as i:
            copy(i * 2, 0)
            copy(i * 2 + 1, 1)
        copy(NB - 1, 0)


def linear(nc, c, name, source, weights, columns, finish, after=None):
    with Stage(nc, name) as st:
        here, here_ready = [st.sb(f"here{s}", [P, D]) for s in range(2)], st.sem("here_ready")
        turned = [st.sb(f"turned{s}", [P, 2, P]) for s in range(2)]
        flips = [st.ps(f"flips{s}", [P, 2, P]) for s in range(2)]
        product = [st.ps(f"product{s}", [P, columns]) for s in range(2)]
        flipped, turned_ready, product_ready, product_free = (
            st.sem(x) for x in ("flipped", "turned_ready", "product_ready", "product_free"))
        stored = st.sem("stored")
        block = st.block()
        copy_blocks(block, source, here, here_ready, flipped)

        @block.tensor
        def _(pe):
            def flip(t, s):
                wait(pe, here_ready, t + 1)
                for k in range(2):
                    last = pe.transpose(flips[s][:, k, :], here[s][:, k * P:(k + 1) * P], c.ident[:, :])
                last.then_inc(flipped, 1)

            def multiply(t, s):
                wait(pe, turned_ready, t + 1)
                wait(pe, product_free, t + 1)
                for k in range(2):
                    last = pe.matmul(product[s][:, :], turned[s][:, k, :], weights[:, k, :], start=k == 0,
                                     stop=k == 1)
                last.then_inc(product_ready, 1)

            pe.sem_inc(product_free, 2)
            flip(0, 0)
            with pe.Fori(0, NB // 2) as i:
                flip(i * 2 + 1, 1)
                multiply(i * 2, 0)
                flip(i * 2 + 2, 0)
                multiply(i * 2 + 1, 1)
            multiply(NB - 1, 0)

        @block.scalar
        def _(act):
            def turn(t, s):
                wait(act, flipped, t + 1)
                if not (isinstance(t, int) and t < 2):
                    wait(act, product_ready, t)
                act.activation(turned[s][:, :, :], flips[s][:, :, :], ACT.Copy).then_inc(turned_ready, 1)

            turn(0, 0)
            turn(1, 1)
            with act.Fori(1, NB // 2) as i:
                turn(i * 2, 0)
                turn(i * 2 + 1, 1)
            turn(NB - 1, 0)

        @block.vector
        def _(dve):
            def end(t, s):
                wait(dve, product_ready, t + 1)
                finish(dve, t, s, product[s]).then_inc(product_free, 1)

            each_block(dve, end)

        if after is not None:
            @block.sync
            def _(sp):
                sp.wait_ge(product_free, NB + 2)
                after(sp, stored)


def two_layers(nc, c, name, source, w1, b1, chunks, func, w2, finish):
    with Stage(nc, name) as st:
        here, here_ready = [st.sb(f"here{s}", [P, D]) for s in range(2)], st.sem("here_ready")
        turned = [st.sb(f"turned{s}", [P, 2, P]) for s in range(2)]
        hidden = [st.sb(f"hidden{s}", [P, chunks, P]) for s in range(2)]
        flips = st.ps("flips", [P, 2, P])
        before = [st.ps(f"before{s}", [P, chunks, P]) for s in range(2)]
        product = [st.ps(f"product{s}", [P, D]) for s in range(2)]
        flipped, turned_ready, before_ready, hidden_ready, product_ready, product_free = (
            st.sem(x) for x in ("flipped", "turned_ready", "before_ready", "hidden_ready", "product_ready",
                                "product_free"))
        block = st.block()
        copy_blocks(block, source, here, here_ready, flipped)

        @block.tensor
        def _(pe):
            def flip(t, s):
                wait(pe, here_ready, t + 1)
                wait(pe, turned_ready, t + 1)
                for k in range(2):
                    last = pe.transpose(flips[:, k, :], here[s][:, k * P:(k + 1) * P], c.ident[:, :])
                last.then_inc(flipped, 1)

            def up(t, s):
                wait(pe, turned_ready, t + 2)
                for j in range(chunks):
                    for k in range(2):
                        last = pe.matmul(before[s][:, j, :], w1[:, k, j * P:(j + 1) * P], turned[s][:, k, :],
                                         start=k == 0, stop=k == 1)
                last.then_inc(before_ready, 1)

            def down(t, s):
                wait(pe, hidden_ready, t + 1)
                wait(pe, product_free, t + 1)
                for j in range(chunks):
                    last = pe.matmul(product[s][:, :], hidden[s][:, j, :], w2[:, j, :], start=j == 0,
                                     stop=j == chunks - 1)
                last.then_inc(product_ready, 1)

            pe.sem_inc(product_free, 2)
            pe.sem_inc(turned_ready, 1)
            flip(0, 0)
            up(0, 0)
            with pe.Fori(0, NB // 2) as i:
                flip(i * 2 + 1, 1)
                up(i * 2 + 1, 1)
                down(i * 2, 0)
                flip(i * 2 + 2, 0)
                up(i * 2 + 2, 0)
                down(i * 2 + 1, 1)
            down(NB - 1, 0)

        @block.scalar
        def _(act):
            def turn(t, s):
                wait(act, flipped, t + 1)
                act.activation(turned[s][:, :, :], flips[:, :, :], ACT.Copy).then_inc(turned_ready, 1)

            def through(t, s):
                wait(act, before_ready, t + 1)
                for j in range(chunks):
                    last = act.activation(hidden[s][:, j, :], before[s][:, j, :], func, bias=b1[:, j:j + 1])
                last.then_inc(hidden_ready, 1)

            turn(0, 0)
            with act.Fori(0, NB // 2) as i:
                turn(i * 2 + 1, 1)
                through(i * 2, 0)
                turn(i * 2 + 2, 0)
                through(i * 2 + 1, 1)
            through(NB - 1, 0)

        @block.vector
        def _(dve):
            def end(t, s):
                wait(dve, product_ready, t + 1)
                finish(dve, t, s, product[s]).then_inc(product_free, 1)

            each_block(dve, end)


def gather_sum(nc, c, name, o, table, target, weighted):
    with Stage(nc, name) as st:
        index = [st.sb(f"index{h}", [P, GT], I32) for h in range(2)]
        rows = [st.sb(f"rows{h}", [P, GT, D]) for h in range(2)]
        hot = [st.sb(f"hot{h}", [P, GT, P]) for h in range(2)]
        sums = [st.ps(f"sums{s}", [P, D]) for s in range(2)]
        landed = [st.sem(f"landed{h}") for h in range(2)]
        copied, hot_ready, sums_ready, sums_free = (
            st.sem(x) for x in ("copied", "hot_ready", "sums_ready", "sums_free"))
        block = st.block()

        @block.gpsimd
        def _(pool):
            with pool.Fori(0, NG // 2) as i:
                for h in range(2):
                    n = i * 2 + h
                    wait(pool, sums_ready, n * GP + GP)
                    pool.tensor_copy(index[h][:, :], c.index[:, o, bass.ds(n * GT, GT)]).then_inc(copied, 1)
                    wait(pool, copied, n + 1)
                    for u in range(GT):
                        pool.indirect_dma_start(rows[h][:, u, :], None, table,
                                                bass.IndirectOffsetOnAxis(ap=index[h][:, u:u + 1], axis=0)
                                                ).then_inc(landed[h], 16)
            for h in range(2):
                pool.wait_ge(landed[h], 16 * NT // 2)

        @block.vector
        def _(dve):
            dve.memset(target[:, :, :], 0.0).then_inc(sums_free, 2)
            with dve.Fori(0, NG // 2) as i:
                for h in range(2):
                    n = i * 2 + h
                    blocks = [dve.value_load(c.block_i[0:1, o, bass.ds(n * GP + q, 1)], min_val=0, max_val=NB - 1)
                              for q in range(GP)]
                    wait(dve, sums_ready, n * GP + GP)
                    for u in range(GT):
                        t = n * GT + u
                        if weighted:
                            last = dve.tensor_scalar(hot[h][:, u, :], c.count[:, :], c.local[:, o, bass.ds(t, 1)],
                                                     c.weight[:, bass.ds(t, 1)], ALU.is_equal, ALU.mult)
                        else:
                            last = dve.tensor_scalar(hot[h][:, u, :], c.count[:, :], c.local[:, o, bass.ds(t, 1)],
                                                     None, ALU.is_equal)
                    last.then_inc(hot_ready, 1)
                    for q in range(GP):
                        wait(dve, sums_ready, n * GP + q + 1 + 2 * GP)
                        wait(dve, sums_free, n * GP + q + 2)
                        to = at(target, blocks[q])[:, 0:D]
                        dve.tensor_tensor(to, to, sums[q % 2][:, :], ALU.add).then_inc(sums_free, 1)

        @block.tensor
        def _(pe):
            pe.sem_inc(sums_ready, 2 * GP)
            with pe.Fori(0, NG // 2) as i:
                for h in range(2):
                    n = i * 2 + h
                    wait(pe, hot_ready, n + 1)
                    wait(pe, landed[h], i * (16 * GT) + 16 * GT)
                    for q in range(GP):
                        wait(pe, sums_free, n * GP + q + 1)
                        for k in range(2):
                            last = pe.matmul(sums[q % 2][:, :], hot[h][:, 2 * q + k, :], rows[h][:, 2 * q + k, :],
                                             start=k == 0, stop=k == 1)
                        last.then_inc(sums_ready, 1)


def fetch(nc, name, copies):
    with Stage(nc, name) as st:
        landed = st.sem("landed")
        block = st.block()

        @block.sync
        def _(sp):
            for to, source in copies:
                sp.dma_start(to, source).then_inc(landed, 16)
            sp.wait_ge(landed, 16 * len(copies))


def attend(nc, c, name, table, width, values, typed, encode=None):
    index_of = c.typed_index if typed else c.index[:, DST, :]
    with Stage(nc, name) as st:
        index = [st.sb(f"index{h}", [P, GT], I32) for h in range(2)]
        rows = [st.sb(f"rows{h}", [P, GT, width]) for h in range(2)]
        hot = [st.sb(f"hot{h}", [P, GT, P]) for h in range(2)]
        hot_last = [st.sb(f"hot_last{h}", [P, GT, P]) for h in range(2)]
        fresh = [st.sb(f"fresh{h}", [P, GT, H]) for h in range(2)]
        turned = [st.sb(f"turned{h}", [P, GT, P]) for h in range(2)]
        score = [st.sb(f"score{h}", [P, GT, H]) for h in range(2)]
        prods = [st.sb(f"prods{s}", [P, 2, D]) for s in range(2)]
        weighted = [st.sb(f"weighted{s}", [P, 2, VC]) for s in range(2)]
        flat, run = st.sb("flat", [GT * H, 2, P]), st.sb("run", [GT * H, P])
        reach = st.sb("reach", [P, GT, H + 1])
        missing, raised, highest = st.sb("missing", [P, GT]), st.sb("raised", [P, GT, H]), st.sb("highest", [P, GP, H])
        before, shrink = st.sb("before", [P, H]), st.sb("shrink", [P, H])
        below, prob = st.sb("below", [P, GT, H]), st.sb("prob", [P, GT, H])
        flips = st.ps("flips", [P, 2, 2, P])
        query = st.ps("query", [P, 2, 512])
        small = st.ps("small", [P, 512])
        sums = [st.ps(f"sums{s}", [P, VC]) for s in range(2)]
        flat_ps = small[0:GT * H, 0:2 * P].rearrange("p (a e) -> p a e", a=2)
        back_ps = small[:, 256:256 + GT * H].rearrange("p (u h) -> p u h", h=H)
        tops_ps = small[:, 320:320 + GT * (H + 1)].rearrange("p (u h) -> p u h", h=H + 1)
        top_ps = small[:, 392:392 + GT * H].rearrange("p (u h) -> p u h", h=H)
        if not typed:
            fields = [st.sb(f"fields{h}", [P, GT * EF]) for h in range(2)]
            fields_t = st.sb("fields_t", [GT * EF, P])
            code = [st.sb(f"code{s}", [P, 2, D]) for s in range(2)]
            ends = st.sb("ends", [P, GT, H])
            fields_ps, code_ps = st.ps("fields_ps", [GT * EF, P]), st.ps("code_ps", [P, 2, D])
            fields_ready, fields_flipped, fields_turned, coded, code_ready, ends_ready = (
                st.sem(x) for x in ("fields_ready", "fields_flipped", "fields_turned", "coded", "code_ready",
                                    "ends_ready"))
        landed = [st.sem(f"landed{h}") for h in range(2)]
        (copied, hot_ready, flipped, turned_ready, query_ready, query_free, score_ready, flat_ready,
         flat_copied, run_ready, back_ready, reach_ready, tops_ready, topped, top_ready, below_ready, prob_ready,
         weighted_ready, sums_ready, added, step) = (
            st.sem(x) for x in ("copied", "hot_ready", "flipped", "turned_ready", "query_ready",
                                "query_free", "score_ready", "flat_ready", "flat_copied", "run_ready", "back_ready",
                                "reach_ready", "tops_ready", "topped", "top_ready", "below_ready", "prob_ready",
                                "weighted_ready", "sums_ready", "added", "step"))
        block = st.block()

        def blocks_of(eng, n):
            return [eng.value_load(c.block_i[0:1, DST, bass.ds(n * GP + q, 1)], min_val=0, max_val=NB - 1)
                    for q in range(GP)]

        @block.gpsimd
        def _(pool):
            with pool.Fori(0, NG // 2) as i:
                for h in range(2):
                    n = i * 2 + h
                    wait(pool, weighted_ready, n * GP + GP)
                    pool.tensor_copy(index[h][:, :], index_of[:, bass.ds(n * GT, GT)]).then_inc(copied, 1)
                    wait(pool, copied, n + 1)
                    for u in range(GT):
                        pool.indirect_dma_start(rows[h][:, u, :], None, table,
                                                bass.IndirectOffsetOnAxis(ap=index[h][:, u:u + 1], axis=0)
                                                ).then_inc(landed[h], 16)
            for h in range(2):
                pool.wait_ge(landed[h], 16 * NT // 2)

        @block.vector
        def _(dve):
            dve.memset(c.acc[:, :, :], 0.0).then_inc(weighted_ready, 2 * GP)
            dve.memset(c.top[:, :, :], -1.0e9 if typed else -FAR)
            dve.memset(reach[:, :, :], 1.0).then_inc(added, 1)
            with dve.Fori(0, NG // 2) as i:
                for h in range(2):
                    n = i * 2 + h
                    m = n * GP
                    per = 9
                    blocks = blocks_of(dve, n)
                    wait(dve, added, m + 1)
                    for u in range(GT):
                        t = n * GT + u
                        dve.tensor_scalar(hot[h][:, u, :], c.count[:, :], c.local[:, DST, bass.ds(t, 1)], None,
                                          ALU.is_equal)
                        dve.tensor_scalar(hot_last[h][:, u, :], c.count[:, :], c.last[:, bass.ds(t, 1)], None,
                                          ALU.is_equal)
                    dve.tensor_copy(fresh[h][:, :, :], spread(c.fresh[:, bass.ds(n * GT, GT)], 2, H)
                                    ).then_inc(hot_ready, 1)
                    wait(dve, landed[h], i * (16 * GT) + 16 * GT)
                    for q in range(GP):
                        two = slice(2 * q, 2 * q + 2)
                        wait(dve, query_ready, m + q + 1)
                        if typed:
                            dve.tensor_tensor(prods[q % 2][:, :, :], query[:, :, 0:D], rows[h][:, two, 0:D],
                                              ALU.mult).then_inc(query_free, 1)
                        else:
                            dve.tensor_tensor(ends[:, two, :], query[:, :, VC + H:VC + 2 * H],
                                              rows[h][:, two, VC:VC + H], ALU.add)
                            wait(dve, code_ready, m + q + 1)
                            dve.tensor_tensor(
                                prods[q % 2][:, :, :].rearrange("p k (h d) -> p k h d", h=H),
                                query[:, :, 0:VC].rearrange("p k (h d) -> p k h d", h=H)[:, :, :, 0:HD],
                                code[q % 2][:, :, :].rearrange("p k (h d) -> p k h d", h=H), ALU.mult
                            ).then_inc(query_free, 1)
                        wait(dve, query_free, m + q + 2)
                        last = dve.tensor_reduce(score[h][:, two, :].rearrange("p k h -> p (k h)"),
                                                 prods[q % 2][:, :, :].rearrange("p k (h d) -> p (k h) d", h=H),
                                                 AX.X, ALU.add)
                    if typed:
                        last.then_inc(score_ready, 1)
                    else:
                        last.then_inc(ends_ready, 1)
                        wait(dve, ends_ready, n * 3 + 1)
                        dve.tensor_tensor(score[h][:, :, :], score[h][:, :, :], ends[:, :, :],
                                          ALU.add).then_inc(ends_ready, 1)
                        wait(dve, ends_ready, n * 3 + 2)
                        dve.tensor_scalar(below[:, :, :], score[h][:, :, :], 0.2, None, ALU.mult).then_inc(ends_ready, 1)
                        wait(dve, ends_ready, n * 3 + 3)
                        dve.tensor_tensor(score[h][:, :, :], score[h][:, :, :], below[:, :, :],
                                          ALU.max).then_inc(score_ready, 1)
                    wait(dve, flat_copied, n + 1)
                    dve.tensor_tensor_scan(run[:, :], flat[:, 1, :], flat[:, 0, :], -FAR, ALU.add,
                                           ALU.max).then_inc(run_ready, 1)
                    wait(dve, tops_ready, n + 1)
                    dve.tensor_scalar(missing[:, :], tops_ps[:, :, H], -1.0, FAR, ALU.add, ALU.mult).then_inc(step, 1)
                    wait(dve, step, n * per + 1)
                    dve.tensor_tensor(raised[:, :, :], tops_ps[:, :, 0:H], spread(missing[:, :], 2, H),
                                      ALU.add).then_inc(step, 1)
                    wait(dve, step, n * per + 2)
                    pairs = raised[:, :, :].rearrange("p (q k) h -> p q k h", k=2)
                    dve.tensor_tensor(highest[:, :, :], pairs[:, :, 0, :], pairs[:, :, 1, :], ALU.max)
                    dve.tensor_copy(before[:, :], at(c.top, blocks[0])).then_inc(step, 1)
                    for q in range(GP):
                        wait(dve, step, n * per + 3 + q)
                        last = dve.tensor_tensor(at(c.top, blocks[q]), at(c.top, blocks[q]), highest[:, q, :], ALU.max)
                        last.then_inc(step, 1)
                    wait(dve, step, n * per + 7)
                    dve.tensor_tensor(shrink[:, :], before[:, :], at(c.top, blocks[0]),
                                      ALU.subtract).then_inc(topped, 1)
                    wait(dve, top_ready, n + 1)
                    dve.tensor_tensor(below[:, :, :], score[h][:, :, :], top_ps, ALU.subtract).then_inc(step, 1)
                    wait(dve, step, n * per + 8)
                    dve.tensor_scalar(below[:, :, :], below[:, :, :], 0.0, None, ALU.min).then_inc(below_ready, 1)
                    wait(dve, prob_ready, n + 1)
                    to = at(c.acc, blocks[0]).rearrange("p (h d) -> p h d", h=H)
                    dve.tensor_tensor(to, to, spread(shrink[:, :], 2, HC), ALU.mult).then_inc(step, 1)

                    def add(q):
                        wait(dve, sums_ready, m + q + 1)
                        wait(dve, added, m + q + 1)
                        to = at(c.acc, blocks[q])
                        dve.tensor_tensor(to, to, sums[q % 2][:, :], ALU.add).then_inc(added, 1)

                    for q in range(GP):
                        two = slice(2 * q, 2 * q + 2)
                        last = dve.tensor_tensor(
                            weighted[q % 2][:, :, :].rearrange("p k (h d) -> p k h d", h=H),
                            rows[h][:, two, values:values + VC].rearrange("p k (h d) -> p k h d", h=H),
                            spread(prob[:, two, :], 3, HC), ALU.mult)
                        last.then_inc(weighted_ready, 1)
                        if q == 0:
                            wait(dve, step, n * per + 9)
                        else:
                            add(q - 1)
                    add(GP - 1)

        @block.scalar
        def _(act):
            with act.Fori(0, NG // 2) as i:
                for h in range(2):
                    n = i * 2 + h
                    m = n * GP
                    if not typed:
                        act.activation(fields[h][:, :], c.meta[:, bass.ds(n * GT, GT), :].rearrange(
                            "p u f -> p (u f)"), ACT.Copy).then_inc(fields_ready, 1)
                        wait(act, fields_flipped, n + 1)
                        act.activation(fields_t[:, :], fields_ps[:, :], ACT.Copy).then_inc(fields_turned, 1)
                    for q in range(GP):
                        wait(act, flipped, m + q + 1)
                        act.activation(turned[h][:, 2 * q:2 * q + 2, :], flips[:, q % 2, :, :],
                                       ACT.Copy).then_inc(turned_ready, 1)
                        if not typed:
                            wait(act, coded, m + q + 1)
                            act.activation(code[q % 2][:, :, :], code_ps[:, :, :], ACT.Relu).then_inc(code_ready, 1)
                    wait(act, flat_ready, n + 1)
                    act.activation(flat[:, :, :], flat_ps, ACT.Copy).then_inc(flat_copied, 1)
                    wait(act, back_ready, n + 1)
                    wait(act, added, 1)
                    act.activation(reach[:, :, 0:H], back_ps, ACT.Copy).then_inc(reach_ready, 1)
                    wait(act, below_ready, n + 1)
                    act.activation(shrink[:, :], shrink[:, :], ACT.Exp)
                    act.activation(prob[:, :, :], below[:, :, :], ACT.Exp).then_inc(prob_ready, 1)

        @block.tensor
        def _(pe):
            pe.sem_inc(query_free, 1)
            with pe.Fori(0, NG // 2) as i:
                for h in range(2):
                    n = i * 2 + h
                    m = n * GP
                    blocks = blocks_of(pe, n)
                    wait(pe, hot_ready, n + 1)
                    if not typed:
                        wait(pe, fields_ready, n + 1)
                        pe.transpose(fields_ps[:, :], fields[h][:, :], c.ident[:, :]).then_inc(fields_flipped, 1)
                    for q in range(GP):
                        if q >= 2:
                            wait(pe, turned_ready, m + q - 1)
                        for k in range(2):
                            last = pe.transpose(flips[:, q % 2, k, :], hot[h][:, 2 * q + k, :], c.ident[:, :])
                        last.then_inc(flipped, 1)
                        if not typed:
                            if q == 0:
                                wait(pe, fields_turned, n + 1)
                            else:
                                wait(pe, code_ready, m + q)
                            for k in range(2):
                                last = pe.matmul(code_ps[:, k, :], fields_t[:, :], encode[:, 2 * q + k, :], start=True,
                                                 stop=True)
                            last.then_inc(coded, 1)
                        wait(pe, turned_ready, m + q + 1)
                        wait(pe, query_free, m + q + 1)
                        for k in range(2):
                            cols = D if typed else VC + 2 * H
                            last = pe.matmul(query[:, k, 0:cols], turned[h][:, 2 * q + k, :],
                                             at(c.q, blocks[q])[:, 0:cols], start=True, stop=True)
                        last.then_inc(query_ready, 1)
                    wait(pe, score_ready, n + 1)
                    pe.transpose(flat_ps[:, 0, :], score[h][:, :, :].rearrange("p u h -> p (u h)"), c.ident[:, :])
                    pe.transpose(flat_ps[:, 1, :], fresh[h][:, :, :].rearrange("p u h -> p (u h)"),
                                 c.ident[:, :]).then_inc(flat_ready, 1)
                    wait(pe, run_ready, n + 1)
                    pe.transpose(small[:, 256:256 + GT * H], run[:, :], c.ident[0:GT * H, 0:GT * H]
                                 ).then_inc(back_ready, 1)
                    wait(pe, reach_ready, n + 1)
                    for u in range(GT):
                        last = pe.matmul(tops_ps[:, u, :], hot_last[h][:, u, :], reach[:, u, :], start=True, stop=True)
                    last.then_inc(tops_ready, 1)
                    wait(pe, topped, n + 1)
                    for u in range(GT):
                        last = pe.matmul(top_ps[:, u, :], turned[h][:, u, :], at(c.top, blocks[u // 2]), start=True,
                                         stop=True)
                    last.then_inc(top_ready, 1)
                    for q in range(GP):
                        wait(pe, weighted_ready, m + q + 1 + 2 * GP)
                        for k in range(2):
                            last = pe.matmul(sums[q % 2][:, :], hot[h][:, 2 * q + k, :], weighted[q % 2][:, k, :],
                                             start=k == 0, stop=k == 1)
                        last.then_inc(sums_ready, 1)


class Buffers:
    pass


def matrix(w):
    return w.rearrange("(k p) n -> p k n", p=P)


def row(v, n):
    return v.rearrange("(a n) -> a n", a=1)[:, :].broadcast_to([P, n])


def layer0(nc, c, a):
    with Stage(nc, "L0") as st:
        w, w1, w2 = (st.sb(x, [P, 2, D]) for x in ("w", "w1", "w2"))
        b, b2 = st.sb("b", [P, D]), st.sb("b2", [P, D])
        b1 = st.sb("b1", [P, 2])
        fetch(nc, "L0w", [(w[:, :, :], matrix(a["L0_gnn_W"])), (w1[:, :, :], matrix(a["L0_gnn_W1"])),
                          (w2[:, :, :], matrix(a["L0_gnn_W2"])), (b[:, :], row(a["L0_gnn_b"], D)),
                          (b2[:, :], row(a["L0_gnn_b2"], D)), (b1[:, :], a["L0_gnn_b1"])])
        normalize(nc, c, "L0n", c.x, c.h, relu=True)

        def scale(dve, t, s, product):
            return dve.tensor_scalar(at(c.q, t)[:, 0:D], product[:, :], c.dinv[:, SRC, bass.ds(t, 1)] if not
                                     isinstance(t, int) else c.dinv[:, SRC, t:t + 1], None, ALU.mult)

        linear(nc, c, "L0p", c.h, w, D, scale, after=lambda sp, stored: store_table(sp, stored, c))
        gather_sum(nc, c, "L0s", SRC, c.rows256, c.acc, True)
        degree_scale(nc, c, "L0d", SRC, b, False)

        with Stage(nc, "L0o") as so:
            part, mid = so.sb("part", [P, 2, D]), so.sem("mid")

            def end(dve, t, s, product):
                dve.tensor_tensor(part[:, s, :], product[:, :], b2[:, :], ALU.add).then_inc(mid, 1)
                wait(dve, mid, t + 1)
                return dve.tensor_tensor(at(c.x, t), at(c.x, t), part[:, s, :], ALU.add)

            two_layers(nc, c, "L0m", c.h, w1, b1, 2, ACT.Relu, w2, end)


def store_table(sp, stored, c):
    sp.dma_start(c.rows256.rearrange("(b p) d -> p b d", p=P), c.q[:, :, 0:D]).then_inc(stored, 16)
    sp.wait_ge(stored, 16)


def degree_scale(nc, c, name, o, bias, residual):
    with Stage(nc, name) as st:
        done = st.sem("done")
        block = st.block()

        @block.vector
        def _(dve):
            count = [0]

            def then(instruction):
                count[0] += 1
                instruction.then_inc(done, 1)
                dve.wait_ge(done, count[0])

            then(dve.tensor_tensor(c.h[:, :, :], c.acc[:, :, 0:D], c.q[:, :, 0:D], ALU.add))
            then(dve.tensor_tensor(c.h[:, :, :], c.h[:, :, :], spread(c.dinv[:, o, :], 2, D), ALU.mult))
            then(dve.tensor_tensor(c.h[:, :, :], c.h[:, :, :], spread(bias[:, :], 1, NB), ALU.add))
            if residual:
                then(dve.tensor_scalar(c.h[:, :, :], c.h[:, :, :], 0.0, None, ALU.max))
                then(dve.tensor_tensor(c.x[:, :, :], c.x[:, :, :], c.h[:, :, :], ALU.add))


def layer1(nc, c, a):
    with Stage(nc, "L1") as st:
        w, b = st.sb("w", [P, 2, D]), st.sb("b", [P, D])
        fetch(nc, "L1w", [(w[:, :, :], matrix(a["L1_gnn_W"])), (b[:, :], row(a["L1_gnn_b"], D))])
        normalize(nc, c, "L1n", c.x, c.h, relu=True)

        def scale(dve, t, s, product):
            return dve.tensor_scalar(at(c.q, t)[:, 0:D], product[:, :], c.dinv[:, DST, bass.ds(t, 1)] if not
                                     isinstance(t, int) else c.dinv[:, DST, t:t + 1], None, ALU.mult)

        linear(nc, c, "L1p", c.h, w, D, scale, after=lambda sp, stored: store_table(sp, stored, c))
        gather_sum(nc, c, "L1s", DST, c.rows256, c.acc, False)
        degree_scale(nc, c, "L1d", DST, b, True)


def queries_keys_values(nc, c, a, layer, mask):
    types, kinds = a["L2_gnn_W_Q"].shape[1], a["L2_gnn_W_E"].shape[1]
    table = c.kv_rows.rearrange("(y n) w -> n y w", y=kinds)
    with Stage(nc, f"qkv{layer}") as st:
        wqv, wk = st.sb("wqv", [P, 2, types, 2, P]), st.sb("wk", [P, 2, types, P])
        we, scale = st.sb("we", [P, 2, kinds, P]), st.sb("scale", [P, 2, kinds])
        cleared, landed, scaled = st.sem("cleared"), st.sem("landed"), st.sem("scaled")
        with nc.Block() as block:
            @block.vector
            def _(dve):
                dve.memset(wqv[:, :, :, :, :], 0.0)
                dve.memset(wk[:, :, :, :], 0.0)
                dve.memset(we[:, :, :, :], 0.0).then_inc(cleared, 1)
                dve.wait_ge(landed, 16 * 5 * H)
                dve.tensor_scalar(scale[:, :, :], scale[:, :, :], float(HD) ** -0.5, None, ALU.mult).then_inc(scaled, 1)
                dve.wait_ge(scaled, 1)
                dve.tensor_tensor(we[:, :, :, :], we[:, :, :, :], spread(scale[:, :, :], 3, P), ALU.mult)

            @block.sync
            def _(sp):
                sp.wait_ge(cleared, 1)
                for h in range(H):
                    half, r = h // 4, slice(h % 4 * HD, (h % 4 + 1) * HD)
                    for to, name in ((wqv[r, half, :, 0, r], "W_Q"), (wqv[r, half, :, 1, r], "W_V"),
                                     (wk[r, half, :, r], "W_K"), (we[r, half, :, r], "W_E")):
                        sp.dma_start(to, a[f"L2_gnn_{name}"][layer, :, h, :, :].rearrange("t d e -> d t e")
                                     ).then_inc(landed, 16)
                    sp.dma_start(scale[r, half, :], a["L2_gnn_mu"][layer, h:h + 1, :].broadcast_to([HD, kinds])
                                 ).then_inc(landed, 16)

        here = [st.sb(f"here{s}", [P, types, D]) for s in range(2)]
        turned = [st.sb(f"turned{s}", [P, types, 2, P]) for s in range(2)]
        key_t = [st.sb(f"key_t{s}", [P, 2, P]) for s in range(2)]
        key_rows = [st.sb(f"key_rows{s}", [P, kinds, D]) for s in range(2)]
        value_rows = [st.sb(f"value_rows{s}", [P, VC]) for s in range(2)]
        flips = st.ps("flips", [P, types, 2, P])
        both = [st.ps(f"both{s}", [P, 2, 2, P]) for s in range(2)]
        key_ps, typed_ps = st.ps("key_ps", [P, 2, P]), st.ps("typed_ps", [P, 2, 512])
        here_ready, flipped, turned_ready, both_ready, key_ready, key_copied, typed_ready, rows_ready, values_ready = (
            st.sem(x) for x in ("here_ready", "flipped", "turned_ready", "both_ready", "key_ready", "key_copied",
                                "typed_ready", "rows_ready", "values_ready"))
        stored = [st.sem(f"stored{s}") for s in range(2)]
        puts = 1 + kinds
        block = st.block()

        def lagged(early, late):
            def run(eng):
                for t in range(4):
                    early(t, t % 2, t // 2)
                    if t:
                        late(t - 1, (t - 1) % 2, (t - 1) // 2)
                with eng.Fori(2, NB // 2) as i:
                    early(i * 2, 0, i)
                    late(i * 2 - 1, 1, i - 1)
                    early(i * 2 + 1, 1, i)
                    late(i * 2, 0, i)
                early(NB - 1, 0, NB // 2)
                late(NB - 2, 1, NB // 2 - 1)
                late(NB - 1, 0, NB // 2)
            return run

        def first(t):
            return isinstance(t, int) and t < 2

        @block.vector
        def _(dve):
            def part(t, s, i):
                if not first(t):
                    wait(dve, flipped, t - 1)
                for y in range(types):
                    factor = mask[:, y, bass.ds(t, 1)] if not isinstance(t, int) else mask[:, y, t:t + 1]
                    last = dve.tensor_scalar(here[s][:, y, :], at(c.h, t), factor, None, ALU.mult)
                last.then_inc(here_ready, 1)

            def end(t, s, i):
                wait(dve, both_ready, t + 1)
                if not first(t):
                    wait(dve, stored[s], i * (16 * puts))
                dve.tensor_copy(at(c.q, t)[:, 0:D].rearrange("p (a e) -> p a e", a=2), both[s][:, :, 0, :])
                dve.tensor_copy(
                    value_rows[s][:, :].rearrange("p (a h d) -> p a h d", a=2, h=H // 2)[:, :, :, 0:HD],
                    both[s][:, :, 1, :].rearrange("p a (h d) -> p a h d", h=H // 2)).then_inc(values_ready, 1)

            dve.memset(value_rows[0][:, :], 1.0).then_inc(values_ready, 1)
            dve.memset(value_rows[1][:, :], 1.0).then_inc(values_ready, 1)
            dve.wait_ge(values_ready, 2)
            lagged(part, end)(dve)

        @block.scalar
        def _(act):
            def turn(t, s, i):
                wait(act, flipped, t + 1)
                for k in range(2):
                    y = slice(k * types // 2, (k + 1) * types // 2)
                    last = act.activation(turned[s][:, y, :, :], flips[:, y, :, :], ACT.Copy)
                last.then_inc(turned_ready, 1)
                wait(act, key_ready, t + 1)
                act.activation(key_t[s][:, :, :], key_ps[:, :, :], ACT.Copy).then_inc(key_copied, 1)
                wait(act, typed_ready, t + 1)
                if not first(t):
                    wait(act, stored[s], i * (16 * puts))
                for k in range(2):
                    last = act.activation(key_rows[s][:, :, k * P:(k + 1) * P],
                                          typed_ps[:, k, 0:kinds * P].rearrange("p (y e) -> p y e", y=kinds), ACT.Copy)
                last.then_inc(rows_ready, 1)

            lagged(turn, lambda t, s, i: None)(act)

        @block.tensor
        def _(pe):
            def multiply(t, s, i):
                wait(pe, here_ready, t + 1)
                wait(pe, turned_ready, t + 1)
                for y in range(types):
                    for k in range(2):
                        last = pe.transpose(flips[:, y, k, :], here[s][:, y, k * P:(k + 1) * P], c.ident[:, :])
                last.then_inc(flipped, 1)
                wait(pe, turned_ready, t + 2)
                wait(pe, key_copied, t + 1)
                for k in range(2):
                    for y in range(types):
                        last = pe.matmul(key_ps[:, k, :], wk[:, k, y, :], turned[s][:, y, k, :], start=y == 0,
                                         stop=y == types - 1)
                last.then_inc(key_ready, 1)
                wait(pe, values_ready, t + 1)
                for k in range(2):
                    for y in range(types):
                        last = pe.matmul(both[s][:, k, :, :].rearrange("p a e -> p (a e)"), turned[s][:, y, k, :],
                                         wqv[:, k, y, :, :].rearrange("p a e -> p (a e)"), start=y == 0,
                                         stop=y == types - 1)
                last.then_inc(both_ready, 1)
                wait(pe, key_copied, t + 2)
                wait(pe, rows_ready, t + 1)
                for k in range(2):
                    last = pe.matmul(typed_ps[:, k, 0:kinds * P], key_t[s][:, k, :],
                                     we[:, k, :, :].rearrange("p y e -> p (y e)"), start=True, stop=True)
                last.then_inc(typed_ready, 1)

            for free in (turned_ready, key_copied, rows_ready):
                pe.sem_inc(free, 1)
            lagged(multiply, lambda t, s, i: None)(pe)

        @block.sync
        def _(sp):
            def put(t, s, i):
                nodes = bass.ds(t * P, P)
                wait(sp, rows_ready, t + 2)
                wait(sp, values_ready, t + 3)
                sp.dma_start(table[nodes, :, 0:D], key_rows[s][:, :, :]).then_inc(stored[s], 16)
                for y in range(kinds):
                    sp.dma_start(c.kv_rows[bass.ds(t * P + y * NP, P), D:D + VC], value_rows[s][:, :]
                                 ).then_inc(stored[s], 16)

            lagged(put, lambda t, s, i: None)(sp)
            sp.wait_ge(stored[0], 16 * puts * (NB // 2 + 1))
            sp.wait_ge(stored[1], 16 * puts * (NB // 2))


def divide(nc, c, name, floor, finish):
    with Stage(nc, name) as st:
        total = st.sb("total", [P, NB * H])
        done = st.sem("done")
        block = st.block()

        @block.vector
        def _(dve):
            count = [0]

            def then(instruction):
                count[0] += 1
                instruction.then_inc(done, 1)
                dve.wait_ge(done, count[0])

            heads = c.acc[:, :, :].rearrange("p b (h d) -> p (b h) d", h=H)
            then(dve.tensor_scalar(total[:, :], heads[:, :, HD], floor[1], None, floor[0]))
            then(dve.reciprocal(total[:, :], total[:, :]))
            then(dve.tensor_tensor(c.flat[:, :].rearrange("p (n d) -> p n d", d=HD), heads[:, :, 0:HD],
                                   spread(total[:, :], 2, HD), ALU.mult))
            finish(dve, then)


def add_product(c, bias, part, mid):
    def end(dve, t, s, product):
        dve.tensor_tensor(part[:, s, :], product[:, :], bias, ALU.add).then_inc(mid, 1)
        wait(dve, mid, t + 1)
        return dve.tensor_tensor(at(c.h, t), at(c.h, t), part[:, s, :], ALU.add)
    return end


def node_masks(nc, c, a, mask):
    with Stage(nc, "types") as st:
        kind_i, kind = st.sb("kind_i", [P, NB], I32), st.sb("kind", [P, NB])
        cleared, landed, made = st.sem("cleared"), st.sem("landed"), st.sem("made")
        block = st.block()
        full = N // P * P

        @block.sync
        def _(sp):
            sp.wait_ge(cleared, 1)
            sp.dma_start(kind_i[:, 0:NB - 1], a["node_type_4"]).then_inc(landed, 16)
            sp.dma_start(kind_i[0:N - full, NB - 1:NB], a["node_type_4_rest"]).then_inc(landed, 16)

        @block.vector
        def _(dve):
            dve.memset(kind_i[:, :], 0).then_inc(cleared, 1)
            dve.wait_ge(landed, 32)
            dve.tensor_copy(kind[:, :], kind_i[:, :]).then_inc(made, 1)
            dve.wait_ge(made, 1)
            for y in range(mask.shape[1]):
                dve.tensor_scalar(mask[:, y, :], kind[:, :], float(y), None, ALU.is_equal)


def park(nc, c, name, back):
    with Stage(nc, name) as st:
        moved = st.sem("moved")
        block = st.block()

        @block.sync
        def _(sp):
            chip, dram = c.x[:, :, :], c.parked.rearrange("(b p) d -> p b d", p=P)
            sp.dma_start(*((chip, dram) if back else (dram, chip))).then_inc(moved, 16)
            sp.wait_ge(moved, 16)


def layer2(nc, c, a):
    with Stage(nc, "L2") as st:
        types, layers = a["L2_gnn_W_Q"].shape[1], a["L2_gnn_W_Q"].shape[0]
        mask = st.sb("mask", [P, types, NB])
        node_masks(nc, c, a, mask)
        normalize(nc, c, "L2n", c.x, c.h, relu=True)
        park(nc, c, "L2p", False)
        c.q, c.flat = c.x, c.x[:, :, :].rearrange("p b d -> p (b d)")
        for l in range(layers):
            queries_keys_values(nc, c, a, l, mask)
            attend(nc, c, f"L2a{l}", c.kv_rows, D + VC, D, True)
            divide(nc, c, f"L2v{l}", (ALU.add, 1e-10), lambda dve, then: None)
            with Stage(nc, f"L2w{l}") as sw:
                wo, rows = sw.sb("wo", [P, 2, D]), sw.sb("rows", [P, 6, D])
                w1, w2, b1 = sw.sb("w1", [P, 2, 4 * D]), sw.sb("w2", [P, 8, D]), sw.sb("b1", [P, 8])
                part = sw.sb("part", [P, 2, D])
                fetch(nc, f"L2f{l}", [(wo[:, :, :], matrix(a["L2_gnn_Wo"][l])),
                                      (w1[:, :, :], matrix(a["L2_gnn_w1"][l])),
                                      (w2[:, :, :], a["L2_gnn_w2"][l].rearrange("(j p) n -> p j n", p=P)),
                                      (b1[:, :], a["L2_gnn_b1"][l])] +
                      [(rows[:, k, :], row(a[f"L2_gnn_{name}"][l], D)) for k, name in
                       enumerate(("bo", "ln1_g", "ln1_b", "b2", "ln2_g", "ln2_b"))])
                linear(nc, c, f"L2o{l}", c.q, wo, D, add_product(c, rows[:, 0, :], part, sw.sem("mid0")))
                normalize(nc, c, f"L2x{l}", c.h, c.h, gain=rows[:, 1, :], bias=rows[:, 2, :])
                two_layers(nc, c, f"L2m{l}", c.h, w1, b1, 8, ACT.Gelu, w2,
                           add_product(c, rows[:, 3, :], part, sw.sem("mid1")))
                normalize(nc, c, f"L2y{l}", c.h, c.h, gain=rows[:, 4, :], bias=rows[:, 5, :])
        park(nc, c, "L2q", True)
        rows = st.sb("rows", [P, 2, D])
        fetch(nc, "L2g", [(rows[:, 0, :], row(a["L2_gnn_out_g"], D)), (rows[:, 1, :], row(a["L2_gnn_out_b"], D))])
        normalize(nc, c, "L2z", c.h, c.h, gain=rows[:, 0, :], bias=rows[:, 1, :], add_to=c.x)


def layer3(nc, c, a):
    with Stage(nc, "L3") as st:
        w, ends = st.sb("w", [P, 2, D]), st.sb("ends", [P, 2, D])
        with Stage(nc, "L3l") as so:
            part, mid = so.sb("part", [P, 2, 2, D]), so.sem("mid")
            fetch(nc, "L3w", [(w[:, :, :], matrix(a["L3_gnn_W"])),
                              (ends[:, 0, :], row(a["L3_gnn_a_src"].rearrange("h d -> (h d)"), D)),
                              (ends[:, 1, :], row(a["L3_gnn_a_dst"].rearrange("h d -> (h d)"), D))])
            normalize(nc, c, "L3n", c.x, c.h, relu=True)
            with Stage(nc, "L3o") as sx:
                block = sx.block()

                @block.vector
                def _(dve):
                    dve.memset(c.q[:, :, :], 1.0)

            def end(dve, t, s, product):
                q = at(c.q, t)
                dve.tensor_copy(q[:, 0:VC].rearrange("p (h d) -> p h d", h=H)[:, :, 0:HD],
                                product[:, :].rearrange("p (h d) -> p h d", h=H))
                dve.tensor_tensor(part[:, s, :, :], spread(product[:, :], 1, 2), ends[:, :, :], ALU.mult
                                  ).then_inc(mid, 1)
                wait(dve, mid, t + 1)
                return dve.tensor_reduce(q[:, VC:VC + 2 * H],
                                         part[:, s, :, :].rearrange("p a (h d) -> p (a h) d", h=H), AX.X, ALU.add)

            def store(sp, stored):
                sp.dma_start(c.feature_rows.rearrange("(b p) d -> p b d", p=P), c.q[:, :, 0:VC + H]
                             ).then_inc(stored, 16)
                sp.wait_ge(stored, 16)

            linear(nc, c, "L3p", c.h, w, D, end, after=store)
    with Stage(nc, "L3e") as st:
        encode = st.sb("encode", [GT * EF, GT, D])
        with Stage(nc, "L3c") as so:
            cleared, landed = so.sem("cleared"), so.sem("landed")
            block = so.block()

            @block.vector
            def _(dve):
                dve.memset(encode[:, :, :], 0.0).then_inc(cleared, 1)

            @block.sync
            def _(sp):
                sp.wait_ge(cleared, 1)
                for u in range(GT):
                    sp.dma_start(encode[u * EF + 4:u * EF + 7, u, :], a["L3_gnn_edge_W"]).then_inc(landed, 16)
                    sp.dma_start(encode[u * EF + 7:u * EF + 8, u, :], a["L3_gnn_edge_b"].rearrange("(a n) -> a n", a=1)
                                 ).then_inc(landed, 16)
                sp.wait_ge(landed, 16 * 2 * GT)

        attend(nc, c, "L3a", c.feature_rows, VC + H, 0, False, encode)
    with Stage(nc, "L3b") as st:
        bias = st.sb("bias", [P, D])
        fetch(nc, "L3d", [(bias[:, :], row(a["L3_gnn_bias"], D))])
        c.flat = c.h[:, :, :].rearrange("p b d -> p (b d)")

        def finish(dve, then):
            then(dve.tensor_tensor(c.h[:, :, :], c.h[:, :, :], spread(bias[:, :], 1, NB), ALU.add))
            then(dve.tensor_tensor(c.x[:, :, :], c.x[:, :, :], c.h[:, :, :], ALU.add))

        divide(nc, c, "L3v", (ALU.max, 1e-10), finish)


def program(nc, a, out):
    c = Buffers()
    with ExitStack() as ctx:
        def sb(name, shape, dt=F32):
            return ctx.enter_context(nc.sbuf_tensor(name, shape, dt))

        c.ident, c.down, c.up, c.zeros, c.ones, c.upper, c.count = (
            sb(name, [P, P]) for name in ("ident", "down", "up", "zeros", "ones", "upper", "count"))
        c.starts = sb("starts", [P, NB + 1])
        c.x = sb("x", [P, NB, D])
        c.dinv = sb("dinv", [P, 2, NB])
        c.block, c.block_i = sb("block", [P, 2, NPR]), sb("block_i", [P, 2, NPR], I32)
        c.local, c.index = sb("local", [P, 2, NT]), sb("index", [P, 2, NT], I32)
        c.weight, c.typed_index = sb("weight", [P, NT]), sb("typed_index", [P, NT], I32)
        c.last, c.fresh = sb("last", [P, NT]), sb("fresh", [P, NT])
        c.meta = sb("meta", [P, NT, EF])
        c.edge_rows = nc.dram_tensor("edge_rows", [ER, EF], F32, kind="Internal").ap()
        c.source_rows = nc.dram_tensor("source_rows", [ER, SF], F32, kind="Internal").ap()
        c.kv_rows = nc.dram_tensor("kv_rows", [3 * NP, D + VC], F32, kind="Internal").ap()
        c.feature_rows = nc.dram_tensor("feature_rows", [NP, VC + H], F32, kind="Internal").ap()
        c.parked = nc.dram_tensor("parked", [NP, D], F32, kind="Internal").ap()
        c.rows256 = nc.dram_tensor("rows256", [NP, D], F32, kind="Internal").ap()
        with ExitStack() as prep:
            def psb(name, shape, dt=F32):
                return prep.enter_context(nc.sbuf_tensor(name, shape, dt))

            c.turns, c.edge = psb("turns", [P, NPR]), psb("edge", [P, T])
            c.pack, c.first = psb("pack", [P, T, EF]), psb("first", [P, 2, NB + 1])
            c.start_i = psb("start_i", [P, 2, NPR], I32)
            c.place, c.by_source = psb("place", [P, T], I32), psb("by_source", [P, T, SF])
            constants(nc, c)
            load_edges(nc, c, a)
            pair_tables(nc, c)
            rank_sources(nc, c)
            scatter_sources(nc, c)
            load_pairs(nc, c)
        c.h, c.acc, c.top = sb("h", [P, NB, D]), sb("acc", [P, NB, VC]), sb("top", [P, NB, H])
        load_nodes(nc, c, a["x"])
        with nc.sbuf_tensor("features", [P, NB, VC + 2 * H], F32) as c.q:
            layer0(nc, c, a)
            layer1(nc, c, a)
        layer2(nc, c, a)
        with nc.sbuf_tensor("features3", [P, NB, VC + 2 * H], F32) as c.q:
            layer3(nc, c, a)
        store_nodes(nc, c, out)





def load_nodes(nc, c, x):
    with Stage(nc, "load") as st:
        cleared, landed = st.sem("cleared"), st.sem("landed")
        block = st.block()

        @block.vector
        def _(dve):
            dve.memset(c.x[:, NB - 1, :], 0.0).then_inc(cleared, 1)

        @block.sync
        def _(sp):
            full = N // P * P
            sp.dma_start(c.x[:, 0:NB - 1, :], x[0:full, :].rearrange("(b p) d -> p b d", p=P)).then_inc(landed, 16)
            sp.wait_ge(cleared, 1)
            sp.dma_start(c.x[0:N - full, NB - 1, :], x[full:N, :]).then_inc(landed, 16)
            sp.wait_ge(landed, 32)


def store_nodes(nc, c, out):
    with Stage(nc, "store") as st:
        stored = st.sem("stored")
        block = st.block()

        @block.sync
        def _(sp):
            full = N // P * P
            sp.dma_start(out[0:full, :].rearrange("(b p) d -> p b d", p=P), c.x[:, 0:NB - 1, :]).then_inc(stored, 16)
            sp.dma_start(out[full:N, :], c.x[0:N - full, NB - 1, :]).then_inc(stored, 16)
            sp.wait_ge(stored, 32)


def kernel(**inputs):
    import numpy as np
    import concourse.bacc as bacc
    from concourse.bass_utils import run_bass_kernel_spmd

    nc = bacc.Bacc("TRN2", target_bir_lowering=False, num_devices=1)
    arrays, a = {}, {}
    for name, value in inputs.items():
        value = np.asarray(value)
        if name == "L3_gnn_W" or name == "L3_gnn_edge_W":
            value = value.T
        if name == "L0_gnn_b1":
            value = value.reshape(2, P).T
        if name == "L2_gnn_b1":
            value = value.reshape(3, 8, P).transpose(0, 2, 1)
        if name == "node_type_4":
            full = N // P * P
            rest, value = np.ascontiguousarray(value[full:].reshape(-1, 1)), value[:full].reshape(-1, P).T
            arrays["rest_in"] = rest
            a["node_type_4_rest"] = nc.dram_tensor("rest_in", rest.shape, I32, kind="ExternalInput").ap()
        value = np.ascontiguousarray(value)
        arrays[f"{name}_in"] = value
        a[name] = nc.dram_tensor(f"{name}_in", value.shape, mybir.dt.from_np(value.dtype), kind="ExternalInput").ap()
    out = nc.dram_tensor("out", (N, D), F32, kind="ExternalOutput").ap()
    program(nc, a, out)
    return run_bass_kernel_spmd(nc, [arrays], core_ids=[0]).results[0]["out"]
```

```python
import concourse.bass as bass
from concourse import mybir
from contextlib import ExitStack

F32 = mybir.dt.float32
I32 = mybir.dt.int32
ALU = mybir.AluOpType
ACT = mybir.ActivationFunctionType
AX = mybir.AxisListType

P = 128
N = 3125
NB = 25
NP = NB * P
D = 256
H = 8
HD = D // H
HC = HD + 1
VC = H * HC
E = 53125
T = 418
ER = P * T
EF = 8
SF = 4
PAIR = 2 * P
NPR = (E + NB * (PAIR - 1)) // PAIR
GP = 4
GT = 2 * GP
NG = NPR // GP
S = 3
NT = 2 * NPR
U = 5
BIG = float(1 << 20)
FAR = 1.0e30
SRC, DST = 0, 1
assert NPR % (2 * GP) == 0 and NG % S == 1 and NB % U == 0 and T % 22 == 0


def wait(eng, sem, value):
    if isinstance(value, int) and value <= 0:
        return
    eng.wait_ge(sem, value)
    if not isinstance(value, int):
        eng.nop(nofuse=True)


def at(tensor, index):
    if isinstance(index, int):
        return tensor[:, index, :]
    return tensor[:, bass.ds(index, 1), :].rearrange("p a b -> p (a b)")


def spread(ap, axis, count):
    shape = list(ap.shape)
    shape.insert(axis, count)
    return ap.unsqueeze(axis).broadcast_to(shape)


def load_blocks(nc, engine, c, o, first, count):
    _, blocks = nc.values_load_multi_w_load_instructions(
        c.block_i[0:1, o, bass.ds(first + GP, count)], engines=[engine], min_val=0, max_val=NB - 1,
        skip_runtime_bounds_check_because="the table of blocks holds none above NB - 1")
    return blocks


class Stage:

    def __init__(self, nc, name):
        self.nc, self.name, self.stack, self.sems = nc, name, ExitStack(), []

    def __enter__(self):
        return self

    def __exit__(self, *args):
        self.stack.close()
        numbers = sorted(x.num for x in self.sems)
        while numbers:
            end = next((k for k in range(1, len(numbers)) if numbers[k] != numbers[0] + k), len(numbers))
            self.nc.gpsimd.dma_reset(range(numbers[0], numbers[0] + end))
            self.nc.gpsimd.sem_clear(range(numbers[0], numbers[0] + end))
            numbers = numbers[end:]

    def sb(self, name, shape, dt=F32):
        return self.stack.enter_context(self.nc.sbuf_tensor(f"{self.name}_{name}", shape, dt))

    def ps(self, name, shape, dt=F32):
        return self.stack.enter_context(self.nc.psum_tensor(f"{self.name}_{name}", shape, dt))

    def sem(self, name):
        self.sems.append(self.stack.enter_context(self.nc.semaphore(f"{self.name}_{name}")))
        return self.sems[-1]

    def block(self):
        return self.stack.enter_context(self.nc.Block())


def constants(nc, c):
    with Stage(nc, "const") as st:
        filled, counted, made = st.sem("filled"), st.sem("counted"), st.sem("made")
        count_i, turns_i = st.sb("count_i", [P, P], I32), st.sb("turns_i", [P, NPR], I32)
        edge_i = st.sb("edge_i", [P, T], I32)
        block = st.block()

        @block.gpsimd
        def _(pool):
            for t in (c.ident, c.down, c.up, c.zeros):
                pool.memset(t[:, :], 0.0).then_inc(filled, 1)
            for t in (c.ones, c.upper):
                pool.memset(t[:, :], 1.0).then_inc(filled, 1)
            pool.iota(count_i[:, :], pattern=[[1, P]], base=0, channel_multiplier=0)
            pool.iota(turns_i[:, :], pattern=[[1, NPR]], base=0, channel_multiplier=0)
            pool.iota(edge_i[:, :], pattern=[[1, T]], base=0, channel_multiplier=T).then_inc(counted, 1)
            pool.wait_ge(filled, 6)
            for t, base in ((c.ident, 0), (c.down, -1), (c.up, 1)):
                pool.affine_select(out=t[:, :], in_=t[:, :], compare_op=ALU.not_equal, fill=1.0, base=base,
                                   pattern=[[-1, P]], channel_multiplier=1)
            pool.affine_select(out=c.upper[:, :], in_=c.upper[:, :], compare_op=ALU.is_gt, fill=0.0, base=0,
                               pattern=[[1, P]], channel_multiplier=-1)

        @block.vector
        def _(dve):
            dve.wait_ge(counted, 1)
            dve.tensor_copy(c.count[:, :], count_i[:, :])
            dve.tensor_copy(c.turns[:, :], turns_i[:, :])
            dve.tensor_copy(c.edge[:, :], edge_i[:, :]).then_inc(made, 1)


def load_edges(nc, c, a):
    with Stage(nc, "edges") as st:
        ints = [st.sb(f"int{k}", [P, T], I32) for k in range(3)]
        weight, attr = st.sb("weight", [P, T]), st.sb("attr", [P, T, 3])
        junk = st.sb("junk", [P, T])
        less = st.sb("less", [P, 2, NB + 1])
        total = st.ps("total", [P, 2, NB + 1])
        cleared, landed, packed, counted, summed, stored = (
            st.sem(x) for x in ("cleared", "landed", "packed", "counted", "summed", "stored"))
        block = st.block()
        whole = E // T
        cut = whole // 16 * 16

        @block.sync
        def _(sp):
            sp.wait_ge(cleared, 1)
            for to, source, w in ((ints[0], a["src"], 1), (ints[1], a["dst"], 1), (ints[2], a["edge_type_3"], 1),
                                  (weight, a["edge_weight"], 1), (attr, a["edge_attr_3"], 3)):
                flat = source if w == 1 else source.rearrange("e k -> (e k)")
                to = to[:, :] if w == 1 else to[:, :, :].rearrange("p t k -> p (t k)")
                rows = flat[0:whole * T * w].rearrange("(p t) -> p t", t=T * w)
                rest = flat[whole * T * w:E * w].rearrange("(p t) -> p t", p=1)
                sp.dma_start(to[0:cut, :], rows[0:cut, :]).then_inc(landed, 16)
                sp.dma_start(to[cut:whole, :], rows[cut:whole, :]).then_inc(landed, 16)
                sp.dma_start(to[whole:whole + 1, 0:(E - whole * T) * w], rest).then_inc(landed, 16)
            sp.wait_ge(packed, 1)
            sp.dma_start(c.edge_rows.rearrange("(p t) f -> p (t f)", t=T),
                         c.pack[:, :, :].rearrange("p t f -> p (t f)")).then_inc(stored, 16)
            sp.wait_ge(stored, 16)

        @block.vector
        def _(dve):
            dve.memset(ints[0][:, :], 1 << 20)
            dve.memset(ints[1][:, :], 1 << 20)
            dve.memset(ints[2][:, :], 0)
            dve.memset(weight[:, :], 0.0)
            dve.memset(c.pack[:, :, 7], 1.0)
            dve.memset(attr[:, :, :], 0.0).then_inc(cleared, 1)
            dve.wait_ge(landed, 15 * 16)
            for k in range(3):
                dve.tensor_copy(c.pack[:, :, k], ints[k][:, :])
            dve.tensor_copy(c.pack[:, :, 3], weight[:, :])
            dve.tensor_copy(c.pack[:, :, 4:7], attr[:, :, :]).then_inc(packed, 1)
            dve.wait_ge(packed, 1)
            for b in range(NB + 1):
                for o in (SRC, DST):
                    n = 2 * b + o
                    if n:
                        dve.wait_ge(counted, n)
                    dve.tensor_scalar(junk[:, :], c.pack[:, :, o], float(P * b), 0.0, ALU.is_lt, ALU.add,
                                      accum_out=less[:, o, b:b + 1]).then_inc(counted, 1)
            dve.wait_ge(summed, 1)
            dve.tensor_copy(c.first[:, :, :], total[:, :, :])

        @block.tensor
        def _(pe):
            pe.wait_ge(counted, 2 * (NB + 1))
            pe.matmul(total[:, :, :].rearrange("p o b -> p (o b)"), c.ones[:, :],
                      less[:, :, :].rearrange("p o b -> p (o b)"), start=True, stop=True).then_inc(summed, 1)


def count_pairs(st, c, dve, then):
    size, size_i, nothing = st.sb("size", [P, 2, NB]), st.sb("size_i", [P, 2, NB], I32), st.sb("nil", [P, NB])
    dve.memset(nothing[:, :], 0.0)
    dve.memset(c.before[:, :, 0], 0.0)
    then(dve.tensor_tensor(size[:, :, :], c.first[:, :, 1:], c.first[:, :, :NB], ALU.subtract))
    then(dve.tensor_scalar(size_i[:, :, :], size[:, :, :], float(PAIR - 1), None, ALU.add))
    then(dve.tensor_scalar(size_i[:, :, :], size_i[:, :, :], 8, None, ALU.arith_shift_right))
    then(dve.tensor_copy(size[:, :, :], size_i[:, :, :]))
    for o in (SRC, DST):
        then(dve.tensor_tensor_scan(c.before[:, o, 1:], size[:, o, :], nothing[:, :], 0.0, ALU.add, ALU.add))


def pair_tables(st, c):
    offset, step = st.sb("offset", [P, NB + 1]), st.sb("step", [P, NB + 1])
    reached, stepped = st.sb("reached", [P, NPR, NB + 1]), st.sb("stepped", [P, NPR, NB + 1])
    start = st.sb("start", [P, NPR])
    done, tables_ready = st.sem("done"), st.sem("tables_ready")

    def steps(dve):
        count = [0]

        def then(instruction):
            count[0] += 1
            instruction.then_inc(done, 1)
            dve.wait_ge(done, count[0])

        then(dve.scalar_tensor_tensor(offset[:, :], c.before[:, DST, :], -float(PAIR), c.first[:, DST, :], ALU.mult,
                                      ALU.add))
        dve.tensor_copy(step[:, 0:1], offset[:, 0:1])
        then(dve.tensor_tensor(step[:, 1:], offset[:, 1:], offset[:, :NB], ALU.subtract))
        then(dve.memset(c.block_i[:, :, :], 0))
        for o in (SRC, DST):
            then(dve.tensor_tensor(reached[:, :, :], spread(c.before[:, o, :], 1, NPR),
                                   spread(c.turns[:, :], 2, NB + 1), ALU.is_le))
            then(dve.tensor_reduce(c.block[:, o, :], reached[:, :, 1:], AX.X, ALU.add))
            then(dve.tensor_scalar(c.block[:, o, :], c.block[:, o, :], float(NB - 1), None, ALU.min))
            dve.tensor_copy(c.block_i[:, o, GP:GP + NPR], c.block[:, o, :])
        then(dve.tensor_tensor(stepped[:, :, :], reached[:, :, :], spread(step[:, :], 1, NPR), ALU.mult))
        then(dve.tensor_reduce(start[:, :], stepped[:, :, :], AX.X, ALU.add))
        then(dve.scalar_tensor_tensor(start[:, :], c.turns[:, :], float(PAIR), start[:, :], ALU.mult, ALU.add))
        then(dve.tensor_scalar(start[:, :], start[:, :], float(E), None, ALU.min))
        dve.tensor_copy(c.start_i[:, :], start[:, :]).then_inc(tables_ready, 1)

    return steps, tables_ready


def fetch_pairs(nc, sp, c, landed):
    K = 8
    with sp.Fori(0, NPR // K) as i:
        _, starts = nc.values_load_multi_w_load_instructions(
            c.start_i[0:1, bass.ds(i * K, K)], engines=[mybir.EngineType.SP], min_val=0, max_val=E,
            skip_runtime_bounds_check_because="the table of starts holds none above E")
        for k in range(K):
            sp.dma_start(c.meta[:, bass.ds((i * K + k) * 2, 2), :].rearrange("p k f -> p (k f)"),
                         c.edge_rows[bass.ds(starts[k], PAIR), :].rearrange("(p k) f -> p (k f)", k=2)
                         ).then_inc(landed, 16)


def rank_sources(nc, c):
    with Stage(nc, "rank") as st:
        key, key_i = st.sb("key", [P, T]), st.sb("key_i", [P, T], I32)
        one, many, part = st.sb("one", [P, T]), st.sb("many", [P, T]), st.sb("part", [P, T])
        nothing, place = st.sb("nothing", [P, T]), st.sb("place", [P, T])
        held, base = st.sb("held", [P, NB]), st.sb("base", [P, NB])
        above = st.ps("above", [P, NB])
        done, held_ready, above_ready = st.sem("done"), st.sem("held_ready"), st.sem("above_ready")
        block = st.block()

        @block.vector
        def _(dve):
            count = [0]

            def then(instruction):
                count[0] += 1
                instruction.then_inc(done, 1)
                dve.wait_ge(done, count[0])

            count_pairs(st, c, dve, then)
            dve.memset(nothing[:, :], 0.0)
            then(dve.tensor_copy(key_i[:, :], c.pack[:, :, SRC]))
            then(dve.tensor_scalar(key_i[:, :], key_i[:, :], 7, None, ALU.arith_shift_right))
            then(dve.tensor_copy(key[:, :], key_i[:, :]))
            then(dve.tensor_scalar(part[:, :], c.edge[:, :], float(NPR * PAIR - E), None, ALU.add))
            then(dve.scalar_tensor_tensor(place[:, :], c.edge[:, :], float(E), part[:, :], ALU.is_ge, ALU.mult))
            for b in range(NB):
                then(dve.tensor_scalar(one[:, :], key[:, :], float(b), None, ALU.is_equal))
                then(dve.tensor_tensor_scan(many[:, :], one[:, :], nothing[:, :], 0.0, ALU.add, ALU.add))
                dve.tensor_copy(held[:, b:b + 1], many[:, T - 1:T])
                then(dve.tensor_tensor(part[:, :], one[:, :], many[:, :], ALU.mult))
                then(dve.tensor_tensor(place[:, :], place[:, :], part[:, :], ALU.add))
            dve.drain().then_inc(held_ready, 1)
            dve.wait_ge(above_ready, 1)
            then(dve.tensor_scalar(base[:, :], above[:, :], -1.0, None, ALU.add))
            then(dve.scalar_tensor_tensor(base[:, :], c.before[:, SRC, :NB], float(PAIR), base[:, :], ALU.mult,
                                          ALU.add))
            for b in range(NB):
                then(dve.tensor_scalar(part[:, :], key[:, :], float(b), base[:, b:b + 1], ALU.is_equal, ALU.mult))
                then(dve.tensor_tensor(place[:, :], place[:, :], part[:, :], ALU.add))
            dve.tensor_copy(c.place[:, :], place[:, :])
            dve.tensor_copy(c.by_source[:, :, 0], c.pack[:, :, 1])
            dve.tensor_copy(c.by_source[:, :, 1], c.pack[:, :, 0])
            dve.tensor_copy(c.by_source[:, :, 2], c.pack[:, :, 3])
            dve.tensor_copy(c.by_source[:, :, 3], c.pack[:, :, 7])

        @block.tensor
        def _(pe):
            pe.wait_ge(held_ready, 1)
            pe.matmul(above[:, :], c.upper[:, :], held[:, :], start=True, stop=True).then_inc(above_ready, 1)


def scatter_sources(nc, c):
    B = T // 22
    C = 11
    with Stage(nc, "scatter") as st:
        place = [st.sb(f"place{h}", [P, B], I32) for h in range(2)]
        rows = [st.sb(f"rows{h}", [P, B, SF]) for h in range(2)]
        high_i, high, low = st.sb("high_i", [P, 2, T], I32), st.sb("high", [P, 2, T]), st.sb("low", [P, 2, T])
        lows = [st.sb(f"lows{h}", [P, 2, C, P]) for h in range(2)]
        highs = [st.sb(f"highs{h}", [P, 2, C, NB]) for h in range(2)]
        blank = st.sb("blank", [P, NT * SF])
        sums = [st.ps(f"sums{o}", [P, NB]) for o in range(2)]
        degree, seen = st.sb("degree", [P, 2, NB]), st.sb("seen", [P, 2, NB])
        copied, made, blanked = st.sem("copied"), st.sem("made"), st.sem("blanked")
        stored = [st.sem(f"stored{h}") for h in range(2)]
        split, marked, hot, used, summed = (st.sem(x) for x in ("split", "marked", "hot", "used", "summed"))
        safe, rooted, landed = st.sem("safe"), st.sem("rooted"), st.sem("landed")
        tabulate, tables_ready = pair_tables(st, c)
        block = st.block()

        @block.sync
        def _(sp):
            sp.wait_ge(made, 1)
            sp.dma_start(c.source_rows[0:NPR * PAIR, :].rearrange("(p t) f -> p (t f)", p=P), blank[:, :]
                         ).then_inc(blanked, 16)
            sp.wait_ge(tables_ready, 1)
            fetch_pairs(nc, sp, c, landed)
            sp.wait_ge(landed, 16 * NPR)

        @block.gpsimd
        def _(pool):
            def scatter(i, h):
                col = (i * 2 + h) * B
                if not isinstance(i, int):
                    wait(pool, stored[h], i * (16 * B))
                pool.tensor_copy(place[h][:, :], c.place[:, bass.ds(col, B)])
                pool.tensor_copy(rows[h][:, :, :], c.by_source[:, bass.ds(col, B), :]).then_inc(copied, 1)
                wait(pool, copied, i * 2 + h + 1)
                for k in range(B):
                    pool.indirect_dma_start(c.source_rows, bass.IndirectOffsetOnAxis(ap=place[h][:, k:k + 1], axis=0),
                                            rows[h][:, k, :], None).then_inc(stored[h], 16)

            pool.wait_ge(blanked, 16)
            scatter(0, 0)
            scatter(0, 1)
            with pool.Fori(1, T // (2 * B)) as i:
                scatter(i, 0)
                scatter(i, 1)
            for h in range(2):
                pool.wait_ge(stored[h], 16 * B * (T // (2 * B)))

        @block.vector
        def _(dve):
            dve.memset(blank[:, :], BIG).then_inc(made, 1)
            tabulate(dve)
            for o in (SRC, DST):
                dve.tensor_copy(high_i[:, o, :], c.pack[:, :, o]).then_inc(split, 1)
            dve.wait_ge(split, 2)
            dve.tensor_scalar(high_i[:, :, :], high_i[:, :, :], 7, None, ALU.arith_shift_right).then_inc(split, 1)
            dve.wait_ge(split, 3)
            dve.tensor_copy(high[:, :, :], high_i[:, :, :]).then_inc(split, 1)
            dve.wait_ge(split, 4)
            for o in (SRC, DST):
                dve.scalar_tensor_tensor(low[:, o, :], high[:, o, :], -float(P), c.pack[:, :, o], ALU.mult,
                                         ALU.add).then_inc(split, 1)
            dve.wait_ge(split, 6)
            with dve.Fori(0, T // (2 * C)) as i:
                for h in range(2):
                    g = i * 2 + h
                    tiles = bass.ds(g * C, C)
                    wait(dve, used, g + 1)
                    for o in (DST, SRC):
                        dve.tensor_tensor(highs[h][:, o, :, :], spread(c.count[:, :NB], 1, C),
                                          spread(high[:, o, tiles], 2, NB), ALU.is_equal).then_inc(marked, 1)
                        dve.tensor_tensor(lows[h][:, o, :, :], spread(c.count[:, :], 1, C),
                                          spread(low[:, o, tiles], 2, P), ALU.is_equal)
                    wait(dve, marked, g * 2 + 2)
                    dve.tensor_tensor(highs[h][:, SRC, :, :], highs[h][:, SRC, :, :],
                                      spread(c.pack[:, tiles, 3], 2, NB), ALU.mult).then_inc(hot, 1)
            dve.wait_ge(summed, 1)
            for o in (SRC, DST):
                dve.tensor_scalar(degree[:, o, :], sums[o][:, :], 1.0, None, ALU.add).then_inc(safe, 1)
            dve.wait_ge(safe, 2)
            dve.tensor_scalar(seen[:, :, :], degree[:, :, :], 0.0, None, ALU.is_gt)
            dve.tensor_scalar(degree[:, :, :], degree[:, :, :], 1e-30, None, ALU.max).then_inc(safe, 1)
            dve.wait_ge(safe, 3)
            dve.reciprocal(degree[:, :, :], degree[:, :, :]).then_inc(safe, 1)
            dve.wait_ge(rooted, 1)
            dve.tensor_tensor(c.dinv[:, :, :], c.dinv[:, :, :], seen[:, :, :], ALU.mult)

        @block.scalar
        def _(act):
            act.wait_ge(safe, 4)
            act.activation(c.dinv[:, :, :], degree[:, :, :], ACT.Sqrt).then_inc(rooted, 1)

        @block.tensor
        def _(pe):
            for o in (SRC, DST):
                pe.matmul(sums[o][:, :], c.zeros[:, :], c.zeros[:, :NB], start=True, stop=False).then_inc(used, 1)
            with pe.Fori(0, T // (2 * C)) as i:
                for h in range(2):
                    wait(pe, hot, i * 2 + h + 1)
                    for k in range(C):
                        for o in (SRC, DST):
                            last = pe.matmul(sums[o][:, :], lows[h][:, o, k, :], highs[h][:, o, k, :], start=False,
                                             stop=False)
                    last.then_inc(used, 1)
            for o in (SRC, DST):
                last = pe.matmul(sums[o][:, :], c.zeros[:, :], c.zeros[:, :NB], start=False, stop=True)
            last.then_inc(summed, 1)


def load_pairs(nc, c):
    with Stage(nc, "meta") as st:
        rows = st.sb("rows", [P, NT, SF])
        landed, done, shifted = st.sem("landed"), st.sem("done"), st.sem("shifted")
        key = [st.sb(f"key{o}", [P, NT]) for o in range(2)]
        index, edge = st.sb("index", [P, NT]), st.sb("edge", [P, NT])
        other = [st.ps(f"other{k}", [P, NT]) for k in range(2)]
        block = st.block()

        @block.sync
        def _(sp):
            sp.dma_start(rows[:, :, :].rearrange("p (j k) f -> p j (k f)", k=2),
                         c.source_rows[0:NPR * PAIR, :].rearrange("(j p k) f -> p j (k f)", p=P, k=2)
                         ).then_inc(landed, 16)

        @block.vector
        def _(dve):
            count = [0]

            def then(instruction):
                count[0] += 1
                instruction.then_inc(done, 1)
                dve.wait_ge(done, count[0])

            for o, source in ((DST, c.meta), (SRC, rows)):
                if o == SRC:
                    dve.wait_ge(landed, 16)
                then(dve.tensor_scalar(key[o][:, :], source[:, :, 1], 1.0, None, ALU.add))
                then(dve.scalar_tensor_tensor(c.local[:, o, :].rearrange("p (j k) -> p j k", k=2),
                                              spread(c.block[:, o, :], 2, 2), -float(P),
                                              source[:, :, 1].rearrange("p (j k) -> p j k", k=2), ALU.mult, ALU.add))
                then(dve.tensor_scalar(index[:, :], source[:, :, 0], float(NP - 1), None, ALU.min))
                then(dve.tensor_copy(c.index[:, o, :], index[:, :]))
                if o == DST:
                    then(dve.scalar_tensor_tensor(c.typed_index[:, :], c.meta[:, :, 2], float(NP), index[:, :],
                                                  ALU.mult, ALU.add))
            dve.tensor_copy(c.weight[:, :], rows[:, :, 2])
            dve.wait_ge(shifted, 1)
            dve.tensor_tensor(c.last[:, :], other[0][:, :], key[DST][:, :], ALU.not_equal)
            then(dve.tensor_tensor(edge[:, :], other[1][:, :], key[DST][:, :], ALU.not_equal))
            dve.tensor_scalar(c.fresh[:, :], edge[:, :], -FAR, None, ALU.mult)

        @block.tensor
        def _(pe):
            pe.wait_ge(done, 1)
            pe.matmul(other[0][:, :], c.down[:, :], key[DST][:, :], start=True, stop=True)
            pe.matmul(other[1][:, :], c.up[:, :], key[DST][:, :], start=True, stop=True).then_inc(shifted, 1)


def normalize(nc, c, name, source, target, relu=False, gain=None, bias=None, add_to=None):
    with Stage(nc, name) as st:
        stats = st.sb("stats", [P, NB, 6])
        mean, var, gap = st.sb("mean", [P, NB]), st.sb("var", [P, NB]), st.sb("gap", [P, NB])
        scaled = [st.sb(f"scaled{s}", [P, D]) for s in range(U)]
        done, safe, rooted, counted = st.sem("done"), st.sem("safe"), st.sem("rooted"), st.sem("counted")
        centered, gained, biased, ended = (st.sem(x) for x in ("centered", "gained", "biased", "ended"))
        block = st.block()

        @block.vector
        def _(dve):
            count = [0]

            def then(instruction):
                count[0] += 1
                instruction.then_inc(done, 1)
                dve.wait_ge(done, count[0])

            with dve.Fori(0, NB // U) as i:
                for s in range(U):
                    last = dve.bn_stats(at(stats, i * U + s), at(source, i * U + s))
            dve.drain().then_inc(counted, 1)
            dve.wait_ge(counted, 1)
            then(dve.tensor_tensor(mean[:, :], stats[:, :, 1], stats[:, :, 4], ALU.add))
            then(dve.tensor_tensor(gap[:, :], stats[:, :, 1], stats[:, :, 4], ALU.subtract))
            then(dve.tensor_scalar(mean[:, :], mean[:, :], 0.5, None, ALU.mult))
            then(dve.tensor_tensor(gap[:, :], gap[:, :], gap[:, :], ALU.mult))
            then(dve.tensor_tensor(var[:, :], stats[:, :, 2], stats[:, :, 5], ALU.add))
            then(dve.tensor_scalar(var[:, :], var[:, :], 1.0 / D, 1e-5, ALU.mult, ALU.add))
            then(dve.scalar_tensor_tensor(var[:, :], gap[:, :], 0.25, var[:, :], ALU.mult, ALU.add))
            dve.reciprocal(var[:, :], var[:, :]).then_inc(safe, 1)
            dve.wait_ge(rooted, 1)
            dve.sem_inc(ended, U)
            with dve.Fori(0, NB // U) as i:
                own = gain is not None or add_to is not None
                if own:
                    wait(dve, ended, i * U + U)
                for s in range(U):
                    t = i * U + s
                    dve.tensor_scalar(scaled[s][:, :] if own else at(target, t), at(source, t),
                                      mean[:, bass.ds(t, 1)], gap[:, bass.ds(t, 1)], ALU.subtract,
                                      ALU.mult).then_inc(centered, 1)
                wait(dve, centered, i * U + U)
                if relu:
                    for s in range(U):
                        dve.tensor_scalar(at(target, i * U + s), at(target, i * U + s), 0.0, None, ALU.max)
                if gain is not None:
                    for s in range(U):
                        dve.tensor_tensor(scaled[s][:, :], scaled[s][:, :], gain, ALU.mult).then_inc(gained, 1)
                    wait(dve, gained, i * U + U)
                    for s in range(U):
                        to = at(target, i * U + s) if add_to is None else scaled[s][:, :]
                        dve.tensor_tensor(to, scaled[s][:, :], bias, ALU.add).then_inc(
                            ended if add_to is None else biased, 1)
                if add_to is not None:
                    wait(dve, biased, i * U + U)
                    for s in range(U):
                        dve.tensor_tensor(at(add_to, i * U + s), at(add_to, i * U + s), scaled[s][:, :],
                                          ALU.add).then_inc(ended, 1)

        @block.scalar
        def _(act):
            act.wait_ge(safe, 1)
            act.activation(gap[:, :], var[:, :], ACT.Sqrt).then_inc(rooted, 1)


def each_block(eng, body):
    with eng.Fori(0, NB // 2) as i:
        for s in range(2):
            body(i * 2 + s, s)
    body(NB - 1, (NB - 1) % 2)


def copy_blocks(block, source, here, here_ready, flipped):
    @block.gpsimd
    def _(pool):
        def copy(t, s):
            if not (isinstance(t, int) and t < 2):
                wait(pool, flipped, t - 1)
            pool.tensor_copy(here[s][:, :], at(source, t)).then_inc(here_ready, 1)

        copy(0, 0)
        copy(1, 1)
        with pool.Fori(1, NB // 2) as i:
            copy(i * 2, 0)
            copy(i * 2 + 1, 1)
        copy(NB - 1, 0)


def linear(nc, c, name, source, weights, columns, finish, after=None):
    with Stage(nc, name) as st:
        here, here_ready = [st.sb(f"here{s}", [P, D]) for s in range(2)], st.sem("here_ready")
        turned = [st.sb(f"turned{s}", [P, 2, P]) for s in range(2)]
        flips = [st.ps(f"flips{s}", [P, 2, P]) for s in range(2)]
        product = [st.ps(f"product{s}", [P, columns]) for s in range(2)]
        flipped, turned_ready, product_ready, product_free = (
            st.sem(x) for x in ("flipped", "turned_ready", "product_ready", "product_free"))
        stored = st.sem("stored")
        block = st.block()
        copy_blocks(block, source, here, here_ready, flipped)

        @block.tensor
        def _(pe):
            def flip(t, s):
                wait(pe, here_ready, t + 1)
                for k in range(2):
                    last = pe.transpose(flips[s][:, k, :], here[s][:, k * P:(k + 1) * P], c.ident[:, :])
                last.then_inc(flipped, 1)

            def multiply(t, s):
                wait(pe, turned_ready, t + 1)
                wait(pe, product_free, t + 1)
                for k in range(2):
                    last = pe.matmul(product[s][:, :], turned[s][:, k, :], weights[:, k, :], start=k == 0,
                                     stop=k == 1)
                last.then_inc(product_ready, 1)

            pe.sem_inc(product_free, 2)
            flip(0, 0)
            with pe.Fori(0, NB // 2) as i:
                flip(i * 2 + 1, 1)
                multiply(i * 2, 0)
                flip(i * 2 + 2, 0)
                multiply(i * 2 + 1, 1)
            multiply(NB - 1, 0)

        @block.scalar
        def _(act):
            def turn(t, s):
                wait(act, flipped, t + 1)
                if not (isinstance(t, int) and t < 2):
                    wait(act, product_ready, t)
                act.activation(turned[s][:, :, :], flips[s][:, :, :], ACT.Copy).then_inc(turned_ready, 1)

            turn(0, 0)
            turn(1, 1)
            with act.Fori(1, NB // 2) as i:
                turn(i * 2, 0)
                turn(i * 2 + 1, 1)
            turn(NB - 1, 0)

        @block.vector
        def _(dve):
            def end(t, s):
                wait(dve, product_ready, t + 1)
                finish(dve, t, s, product[s]).then_inc(product_free, 1)

            each_block(dve, end)

        if after is not None:
            @block.sync
            def _(sp):
                sp.wait_ge(product_free, NB + 2)
                after(sp, stored)


def two_layers(nc, c, name, source, w1, b1, chunks, func, w2, finish):
    with Stage(nc, name) as st:
        here, here_ready = [st.sb(f"here{s}", [P, D]) for s in range(2)], st.sem("here_ready")
        turned = [st.sb(f"turned{s}", [P, 2, P]) for s in range(2)]
        hidden = [st.sb(f"hidden{s}", [P, chunks, P]) for s in range(2)]
        flips = st.ps("flips", [P, 2, P])
        before = [st.ps(f"before{s}", [P, chunks, P]) for s in range(2)]
        product = [st.ps(f"product{s}", [P, D]) for s in range(2)]
        flipped, turned_ready, before_ready, hidden_ready, product_ready, product_free = (
            st.sem(x) for x in ("flipped", "turned_ready", "before_ready", "hidden_ready", "product_ready",
                                "product_free"))
        block = st.block()
        copy_blocks(block, source, here, here_ready, flipped)

        @block.tensor
        def _(pe):
            def flip(t, s):
                wait(pe, here_ready, t + 1)
                wait(pe, turned_ready, t + 1)
                for k in range(2):
                    last = pe.transpose(flips[:, k, :], here[s][:, k * P:(k + 1) * P], c.ident[:, :])
                last.then_inc(flipped, 1)

            def up(t, s):
                wait(pe, turned_ready, t + 2)
                for j in range(chunks):
                    for k in range(2):
                        last = pe.matmul(before[s][:, j, :], w1[:, k, j * P:(j + 1) * P], turned[s][:, k, :],
                                         start=k == 0, stop=k == 1)
                last.then_inc(before_ready, 1)

            def down(t, s):
                wait(pe, hidden_ready, t + 1)
                wait(pe, product_free, t + 1)
                for j in range(chunks):
                    last = pe.matmul(product[s][:, :], hidden[s][:, j, :], w2[:, j, :], start=j == 0,
                                     stop=j == chunks - 1)
                last.then_inc(product_ready, 1)

            pe.sem_inc(product_free, 2)
            pe.sem_inc(turned_ready, 1)
            flip(0, 0)
            up(0, 0)
            with pe.Fori(0, NB // 2) as i:
                flip(i * 2 + 1, 1)
                up(i * 2 + 1, 1)
                down(i * 2, 0)
                flip(i * 2 + 2, 0)
                up(i * 2 + 2, 0)
                down(i * 2 + 1, 1)
            down(NB - 1, 0)

        @block.scalar
        def _(act):
            def turn(t, s):
                wait(act, flipped, t + 1)
                act.activation(turned[s][:, :, :], flips[:, :, :], ACT.Copy).then_inc(turned_ready, 1)

            def through(t, s):
                wait(act, before_ready, t + 1)
                for j in range(chunks):
                    last = act.activation(hidden[s][:, j, :], before[s][:, j, :], func, bias=b1[:, j:j + 1])
                last.then_inc(hidden_ready, 1)

            turn(0, 0)
            with act.Fori(0, NB // 2) as i:
                turn(i * 2 + 1, 1)
                through(i * 2, 0)
                turn(i * 2 + 2, 0)
                through(i * 2 + 1, 1)
            through(NB - 1, 0)

        @block.vector
        def _(dve):
            def end(t, s):
                wait(dve, product_ready, t + 1)
                finish(dve, t, s, product[s]).then_inc(product_free, 1)

            each_block(dve, end)


def gather_sum(nc, c, name, o, table, target, weighted):
    with Stage(nc, name) as st:
        index = [st.sb(f"index{h}", [P, GT], I32) for h in range(2)]
        rows = [st.sb(f"rows{h}", [P, GT, D]) for h in range(2)]
        hot = [st.sb(f"hot{h}", [P, GT, P]) for h in range(2)]
        sums = [st.ps(f"sums{s}", [P, D]) for s in range(2)]
        landed = [st.sem(f"landed{h}") for h in range(2)]
        copied, hot_ready, sums_ready, sums_free = (
            st.sem(x) for x in ("copied", "hot_ready", "sums_ready", "sums_free"))
        block = st.block()

        @block.gpsimd
        def _(pool):
            with pool.Fori(0, NG // 2) as i:
                for h in range(2):
                    n = i * 2 + h
                    wait(pool, sums_ready, n * GP + GP)
                    pool.tensor_copy(index[h][:, :], c.index[:, o, bass.ds(n * GT, GT)]).then_inc(copied, 1)
                    wait(pool, copied, n + 1)
                    for u in range(GT):
                        pool.indirect_dma_start(rows[h][:, u, :], None, table,
                                                bass.IndirectOffsetOnAxis(ap=index[h][:, u:u + 1], axis=0)
                                                ).then_inc(landed[h], 16)
            for h in range(2):
                pool.wait_ge(landed[h], 16 * NT // 2)

        @block.vector
        def _(dve):
            dve.memset(target[:, :, :], 0.0).then_inc(sums_free, 2)

            def hots(n, h):
                for u in range(GT):
                    t = n * GT + u
                    if weighted:
                        last = dve.tensor_scalar(hot[h][:, u, :], c.count[:, :], c.local[:, o, bass.ds(t, 1)],
                                                 c.weight[:, bass.ds(t, 1)], ALU.is_equal, ALU.mult)
                    else:
                        last = dve.tensor_scalar(hot[h][:, u, :], c.count[:, :], c.local[:, o, bass.ds(t, 1)],
                                                 None, ALU.is_equal)
                last.then_inc(hot_ready, 1)

            def adds(n):
                blocks = load_blocks(nc, mybir.EngineType.DVE, c, o, n * GP, GP)
                for q in range(GP):
                    wait(dve, sums_ready, n * GP + q + 1 + 2 * GP)
                    wait(dve, sums_free, n * GP + q + 2)
                    to = at(target, blocks[q])[:, 0:D]
                    dve.tensor_tensor(to, to, sums[q % 2][:, :], ALU.add).then_inc(sums_free, 1)

            hots(0, 0)
            with dve.Fori(0, NG // 2 - 1) as i:
                hots(i * 2 + 1, 1)
                adds(i * 2)
                hots(i * 2 + 2, 0)
                adds(i * 2 + 1)
            hots(NG - 1, 1)
            adds(NG - 2)
            adds(NG - 1)

        @block.tensor
        def _(pe):
            pe.sem_inc(sums_ready, 2 * GP)
            with pe.Fori(0, NG // 2) as i:
                for h in range(2):
                    n = i * 2 + h
                    wait(pe, hot_ready, n + 1)
                    wait(pe, landed[h], i * (16 * GT) + 16 * GT)
                    for q in range(GP):
                        wait(pe, sums_free, n * GP + q + 1)
                        for k in range(2):
                            last = pe.matmul(sums[q % 2][:, :], hot[h][:, 2 * q + k, :], rows[h][:, 2 * q + k, :],
                                             start=k == 0, stop=k == 1)
                        last.then_inc(sums_ready, 1)


def fetch(nc, name, copies):
    with Stage(nc, name) as st:
        landed = st.sem("landed")
        block = st.block()

        @block.sync
        def _(sp):
            for to, source in copies:
                sp.dma_start(to, source).then_inc(landed, 16)
            sp.wait_ge(landed, 16 * len(copies))


def attend(nc, c, name, table, width, values, typed, encode=None):
    index_of = c.typed_index if typed else c.index[:, DST, :]
    with Stage(nc, name) as st:
        index = [st.sb(f"index{s}", [P, GT], I32) for s in range(S)]
        rows = [st.sb(f"rows{s}", [P, GT, width]) for s in range(S)]
        hot = [st.sb(f"hot{s}", [P, GT, P]) for s in range(S)]
        fresh = [st.sb(f"fresh{s}", [P, GT, H]) for s in range(S)]
        turned = [st.sb(f"turned{s}", [P, GT, P]) for s in range(S)]
        score = [st.sb(f"score{s}", [P, GT, H]) for s in range(S)]
        prods = [st.sb(f"prods{k}", [P, 2, D]) for k in range(2)]
        weighted = [st.sb(f"weighted{q}", [P, 2, VC]) for q in range(GP)]
        flat, run = st.sb("flat", [GT * H, 2, P]), st.sb("run", [GT * H, P])
        reach = st.sb("reach", [P, GT, H + 1])
        missing, raised, highest = st.sb("missing", [P, GT]), st.sb("raised", [P, GT, H]), st.sb("highest", [P, GP, H])
        before, shrink = st.sb("before", [P, H]), st.sb("shrink", [P, H])
        below, prob = st.sb("below", [P, GT, H]), st.sb("prob", [P, GT, H])
        flips = st.ps("flips", [P, GT // 2, P])
        held = GP if typed else 2
        query = [st.ps(f"query{k}", [P, 2, D]) for k in range(held)]
        small = st.ps("small", [P, 512])
        sums = [st.ps(f"sums{k}", [P, VC]) for k in range(2)]
        flat_ps = small[0:GT * H, 0:2 * P].rearrange("p (a e) -> p a e", a=2)
        back_ps = small[:, 256:256 + GT * H].rearrange("p (u h) -> p u h", h=H)
        tops_ps = small[:, 320:320 + GT * (H + 1)].rearrange("p (u h) -> p u h", h=H + 1)
        top_ps = small[:, 392:392 + GT * H].rearrange("p (u h) -> p u h", h=H)
        if not typed:
            fields = st.sb("fields", [P, GT * EF])
            fields_t = st.sb("fields_t", [GT * EF, P])
            code = [st.sb(f"code{k}", [P, 2, D]) for k in range(2)]
            ends = st.sb("ends", [P, GT, H])
            extra, code_ps = st.ps("extra", [P, P + GT * H]), st.ps("code_ps", [P, 2, D])
            fields_ps = extra[0:GT * EF, 0:P]
            ends_ps = extra[:, P:P + GT * H].rearrange("p (u h) -> p u h", h=H)
            fields_ready, fields_flipped, fields_turned, coded, code_ready, ends_ready = (
                st.sem(x) for x in ("fields_ready", "fields_flipped", "fields_turned", "coded", "code_ready",
                                    "ends_ready"))
        landed = [st.sem(f"landed{s}") for s in range(S)]
        (copied, hot_ready, flipped, turned_ready, query_ready, multiplied, score_ready, flat_ready,
         flat_copied, run_ready, back_ready, reach_ready, tops_ready, topped, top_ready, below_ready, prob_ready,
         weighted_ready, sums_ready, added, step) = (
            st.sem(x) for x in ("copied", "hot_ready", "flipped", "turned_ready", "query_ready",
                                "multiplied", "score_ready", "flat_ready", "flat_copied", "run_ready", "back_ready",
                                "reach_ready", "tops_ready", "topped", "top_ready", "below_ready", "prob_ready",
                                "weighted_ready", "sums_ready", "added", "step"))
        block = st.block()

        def two(q):
            return slice(2 * q, 2 * q + 2)

        def pipelined(eng, begin, body):
            begin()
            body(0, 0, 0, 2)
            with eng.Fori(0, (NG - S - 1) // S) as i:
                for k in range(1, S + 1):
                    body(i * S + k, k % S, i + k // S, 2)
            for n in range(NG - S, NG):
                body(n, n % S, n // S, min(NG - 1 - n, 2))

        def after(n, s, i):
            return n + 1, (s + 1) % S, i + (s + 1) // S

        @block.gpsimd
        def _(pool):
            def gather(n, s):
                wait(pool, weighted_ready, (n - (S - 1)) * GP)
                pool.tensor_copy(index[s][:, :], index_of[:, bass.ds(n * GT, GT)]).then_inc(copied, 1)
                wait(pool, copied, n + 1)
                for u in range(GT):
                    pool.indirect_dma_start(rows[s][:, u, :], None, table,
                                            bass.IndirectOffsetOnAxis(ap=index[s][:, u:u + 1], axis=0)
                                            ).then_inc(landed[s], 16)

            for n in range(S):
                gather(n, n)
            with pool.Fori(1, NG // S) as i:
                for s in range(S):
                    gather(i * S + s, s)
            for n in range(NG // S * S, NG):
                gather(n, n % S)
            for s in range(S):
                pool.wait_ge(landed[s], 16 * GT * len(range(s, NG, S)))

        @block.vector
        def _(dve):
            def hots(n, s):
                dve.tensor_tensor(hot[s][:, :, :], spread(c.count[:, :], 1, GT),
                                  spread(c.local[:, DST, bass.ds(n * GT, GT)], 2, P), ALU.is_equal)
                dve.tensor_copy(fresh[s][:, :, :], spread(c.fresh[:, bass.ds(n * GT, GT)], 2, H)
                                ).then_inc(hot_ready, 1)

            def product(n, s, i, q):
                if q == 0:
                    wait(dve, landed[s], i * (16 * GT) + 16 * GT)
                wait(dve, query_ready, n * GP + q + 1)
                if typed:
                    dve.tensor_tensor(prods[q % 2][:, :, :], query[q % held][:, :, :], rows[s][:, two(q), 0:D],
                                      ALU.mult).then_inc(multiplied, 1)
                else:
                    wait(dve, code_ready, n * GP + q + 1)
                    dve.tensor_tensor(prods[q % 2][:, :, :], query[q % held][:, :, :], code[q % 2][:, :, :],
                                      ALU.mult).then_inc(multiplied, 1)

            def reduce(n, s, q):
                wait(dve, multiplied, n * GP + q + 1)
                last = dve.tensor_reduce(score[s][:, two(q), :].rearrange("p k h -> p (k h)"),
                                         prods[q % 2][:, :, :].rearrange("p k (h d) -> p (k h) d", h=H), AX.X, ALU.add)
                if q == GP - 1:
                    if typed:
                        last.then_inc(score_ready, 1)
                    else:
                        dve.tensor_tensor(ends[:, :, :], ends_ps, rows[s][:, :, VC:VC + H], ALU.add
                                          ).then_inc(ends_ready, 1)
                        wait(dve, ends_ready, n * 2 + 1)
                        dve.tensor_tensor(score[s][:, :, :], score[s][:, :, :], ends[:, :, :],
                                          ALU.add).then_inc(ends_ready, 1)
                        wait(dve, ends_ready, n * 2 + 2)
                        dve.scalar_tensor_tensor(score[s][:, :, :], score[s][:, :, :], 0.2, score[s][:, :, :], ALU.mult,
                                                 ALU.max).then_inc(score_ready, 1)

            def add(n, q, b):
                wait(dve, sums_ready, n * GP + q + 1)
                wait(dve, added, n * GP + q)
                dve.tensor_tensor(at(c.acc, b), at(c.acc, b), sums[q % 2][:, :], ALU.add).then_inc(added, 1)

            def begin():
                hots(0, 0)
                hots(1, 1)
                for q in range(GP):
                    product(0, 0, 0, q)
                    reduce(0, 0, q)

            def body(n, s, i, more):
                last_two_and_own = load_blocks(nc, mybir.EngineType.DVE, c, DST, n * GP - 2, GP + 2)
                blocks = last_two_and_own[2:]
                per = 9
                m, s1, i1 = after(n, s, i)
                wait(dve, flat_copied, n + 1)
                dve.tensor_tensor_scan(run[:, :], flat[:, 1, :], flat[:, 0, :], -FAR, ALU.add,
                                       ALU.max).then_inc(run_ready, 1)
                later = not (isinstance(n, int) and n == 0)
                if more:
                    product(m, s1, i1, 0)
                if later:
                    add(n - 1, GP - 2, last_two_and_own[0])
                if more:
                    reduce(m, s1, 0)
                if later:
                    add(n - 1, GP - 1, last_two_and_own[1])
                wait(dve, back_ready, n + 1)
                flags = c.last[:, bass.ds(n * GT, GT)]
                dve.tensor_tensor(reach[:, :, 0:H], back_ps, spread(flags, 2, H), ALU.mult)
                dve.tensor_copy(reach[:, :, H], flags).then_inc(reach_ready, 1)
                if more:
                    product(m, s1, i1, 1)
                if more > 1:
                    hots(n + 2, (s + 2) % S)
                wait(dve, tops_ready, n + 1)
                dve.tensor_scalar(missing[:, :], tops_ps[:, :, H], -1.0, FAR, ALU.add, ALU.mult).then_inc(step, 1)
                wait(dve, step, n * per + 1)
                dve.tensor_tensor(raised[:, :, :], tops_ps[:, :, 0:H], spread(missing[:, :], 2, H),
                                  ALU.add).then_inc(step, 1)
                if more:
                    reduce(m, s1, 1)
                wait(dve, step, n * per + 2)
                pairs = raised[:, :, :].rearrange("p (q k) h -> p q k h", k=2)
                dve.tensor_tensor(highest[:, :, :], pairs[:, :, 0, :], pairs[:, :, 1, :], ALU.max)
                dve.tensor_copy(before[:, :], at(c.top, blocks[0])).then_inc(step, 1)
                for q in range(GP):
                    wait(dve, step, n * per + 3 + q)
                    top = at(c.top, blocks[q])
                    dve.tensor_tensor(top, top, highest[:, q, :], ALU.max).then_inc(step, 1)
                wait(dve, step, n * per + 7)
                dve.tensor_tensor(shrink[:, :], before[:, :], at(c.top, blocks[0]), ALU.subtract).then_inc(topped, 1)
                if more:
                    product(m, s1, i1, 2)
                    product(m, s1, i1, 3)
                wait(dve, top_ready, n + 1)
                dve.tensor_tensor(below[:, :, :], score[s][:, :, :], top_ps, ALU.subtract).then_inc(step, 1)
                if more:
                    reduce(m, s1, 2)
                wait(dve, step, n * per + 8)
                dve.tensor_scalar(below[:, :, :], below[:, :, :], 0.0, None, ALU.min).then_inc(below_ready, 1)
                if more:
                    reduce(m, s1, 3)
                wait(dve, prob_ready, n + 1)
                wait(dve, added, n * GP)
                to = at(c.acc, blocks[0]).rearrange("p (h d) -> p h d", h=H)
                dve.tensor_tensor(to, to, spread(shrink[:, :], 2, HC), ALU.mult).then_inc(step, 1)
                for q in range(GP):
                    dve.tensor_tensor(
                        weighted[q][:, :, :].rearrange("p k (h d) -> p k h d", h=H),
                        rows[s][:, two(q), values:values + VC].rearrange("p k (h d) -> p k h d", h=H),
                        spread(prob[:, two(q), :], 3, HC), ALU.mult).then_inc(weighted_ready, 1)
                    if q == 2:
                        wait(dve, step, n * per + 9)
                    if q >= 2:
                        add(n, q - 2, blocks[q - 2])
                if not more:
                    add(n, GP - 2, blocks[GP - 2])
                    add(n, GP - 1, blocks[GP - 1])

            dve.memset(c.acc[:, :, :], 0.0)
            dve.memset(c.top[:, :, :], -1.0e9 if typed else -FAR)
            pipelined(dve, begin, body)

        @block.scalar
        def _(act):
            def turn(n, s, half):
                wait(act, flipped, n * 2 + half + 1)
                act.activation(turned[s][:, half * GT // 2:(half + 1) * GT // 2, :], flips[:, :, :], ACT.Copy
                               ).then_inc(turned_ready, 1)

            def encoded(n, q):
                if not typed:
                    wait(act, coded, n * GP + q + 1)
                    wait(act, multiplied, n * GP + q - 1)
                    act.activation(code[q % 2][:, :, :], code_ps[:, :, :], ACT.Relu).then_inc(code_ready, 1)

            def turns(n, s):
                turn(n, s, 0)
                turn(n, s, 1)

            def turn_fields(n):
                if not typed:
                    act.activation(fields[:, :], c.meta[:, bass.ds(n * GT, GT), :].rearrange("p u f -> p (u f)"),
                                   ACT.Copy).then_inc(fields_ready, 1)
                    wait(act, fields_flipped, n + 1)
                    act.activation(fields_t[:, :], fields_ps, ACT.Copy).then_inc(fields_turned, 1)

            def level(n):
                wait(act, flat_ready, n + 1)
                act.activation(flat[:, :, :], flat_ps, ACT.Copy).then_inc(flat_copied, 1)

            def begin():
                for n in range(2):
                    turns(n, n)
                    turn_fields(n)
                    for q in range(GP if n == 0 else 2):
                        encoded(n, q)
                    if n == 0:
                        level(0)

            def body(n, s, i, more):
                if more:
                    encoded(n + 1, 2)
                    encoded(n + 1, 3)
                if more > 1:
                    turns(n + 2, (s + 2) % S)
                wait(act, below_ready, n + 1)
                act.activation(shrink[:, :], shrink[:, :], ACT.Exp)
                act.activation(prob[:, :, :], below[:, :, :], ACT.Exp).then_inc(prob_ready, 1)
                if more:
                    level(n + 1)
                if more > 1:
                    turn_fields(n + 2)
                    encoded(n + 2, 0)
                    encoded(n + 2, 1)

            pipelined(act, begin, body)

        @block.tensor
        def _(pe):
            def flip(n, s, half):
                if half == 0:
                    wait(pe, hot_ready, n + 1)
                wait(pe, turned_ready, n * 2 + half)
                for u in range(GT // 2):
                    last = pe.transpose(flips[:, u, :], hot[s][:, half * GT // 2 + u, :], c.ident[:, :])
                last.then_inc(flipped, 1)

            def encode_pair(n, q):
                if not typed:
                    if q == 0:
                        wait(pe, fields_ready, n + 1)
                        pe.transpose(fields_ps, fields[:, :], c.ident[:, :]).then_inc(fields_flipped, 1)
                        wait(pe, fields_turned, n + 1)
                    wait(pe, code_ready, n * GP + q)
                    for k in range(2):
                        last = pe.matmul(code_ps[:, k, :], fields_t[:, :], encode[:, 2 * q + k, :], start=True,
                                         stop=True)
                    last.then_inc(coded, 1)

            def ask(n, s, q, b):
                wait(pe, turned_ready, n * 2 + q // 2 + 1)
                wait(pe, multiplied, n * GP + q + 1 - held)
                for k in range(2):
                    if not typed:
                        pe.matmul(ends_ps[:, 2 * q + k, :], turned[s][:, 2 * q + k, :], at(c.ends, b),
                                  start=True, stop=True)
                    last = pe.matmul(query[q % held][:, k, :], turned[s][:, 2 * q + k, :], at(c.q, b)[:, 0:D], start=True,
                                     stop=True)
                last.then_inc(query_ready, 1)

            def level(n, s):
                wait(pe, score_ready, n + 1)
                pe.transpose(flat_ps[:, 0, :], score[s][:, :, :].rearrange("p u h -> p (u h)"), c.ident[:, :])
                pe.transpose(flat_ps[:, 1, :], fresh[s][:, :, :].rearrange("p u h -> p (u h)"),
                             c.ident[:, :]).then_inc(flat_ready, 1)

            def total(n, s, q):
                wait(pe, weighted_ready, n * GP + q + 1)
                wait(pe, added, n * GP + q - 1)
                for k in range(2):
                    last = pe.matmul(sums[q % 2][:, :], hot[s][:, 2 * q + k, :], weighted[q][:, k, :],
                                     start=k == 0, stop=k == 1)
                last.then_inc(sums_ready, 1)

            def begin():
                blocks = load_blocks(nc, mybir.EngineType.PE, c, DST, 0, 2 * GP)
                for n in range(2):
                    flip(n, n, 0)
                    flip(n, n, 1)
                    for q in range(GP if n == 0 else 2):
                        encode_pair(n, q)
                        ask(n, n, q, blocks[n * GP + q])
                    if n == 0:
                        level(0, 0)

            def body(n, s, i, more):
                blocks = load_blocks(nc, mybir.EngineType.PE, c, DST, n * GP, 3 * GP)
                m, s1, i1 = after(n, s, i)
                s2 = (s + 2) % S
                wait(pe, run_ready, n + 1)
                pe.transpose(small[:, 256:256 + GT * H], run[:, :], c.ident[0:GT * H, 0:GT * H]).then_inc(back_ready, 1)
                if more:
                    encode_pair(m, 2)
                    ask(m, s1, 2, blocks[GP + 2])
                wait(pe, reach_ready, n + 1)
                for u in range(GT):
                    last = pe.matmul(tops_ps[:, u, :], hot[s][:, u, :], reach[:, u, :], start=True, stop=True)
                last.then_inc(tops_ready, 1)
                if more:
                    encode_pair(m, 3)
                    ask(m, s1, 3, blocks[GP + 3])
                if more > 1:
                    flip(n + 2, s2, 0)
                    flip(n + 2, s2, 1)
                    if typed:
                        ask(n + 2, s2, 0, blocks[2 * GP])
                wait(pe, topped, n + 1)
                for u in range(GT):
                    last = pe.matmul(top_ps[:, u, :], turned[s][:, u, :], at(c.top, blocks[u // 2]), start=True,
                                     stop=True)
                last.then_inc(top_ready, 1)
                if more:
                    level(m, s1)
                for q in range(GP):
                    total(n, s, q)
                    if more > 1 and q < 2:
                        encode_pair(n + 2, q)
                        if q or not typed:
                            ask(n + 2, s2, q, blocks[2 * GP + q])

            pipelined(pe, begin, body)


class Buffers:
    pass


def matrix(w):
    return w.rearrange("(k p) n -> p k n", p=P)


def row(v, n):
    return v.rearrange("(a n) -> a n", a=1)[:, :].broadcast_to([P, n])


def layer0(nc, c, a):
    with Stage(nc, "L0") as st:
        w, w1, w2 = (st.sb(x, [P, 2, D]) for x in ("w", "w1", "w2"))
        b, b2 = st.sb("b", [P, D]), st.sb("b2", [P, D])
        b1 = st.sb("b1", [P, 2])
        fetch(nc, "L0w", [(w[:, :, :], matrix(a["L0_gnn_W"])), (w1[:, :, :], matrix(a["L0_gnn_W1"])),
                          (w2[:, :, :], matrix(a["L0_gnn_W2"])), (b[:, :], row(a["L0_gnn_b"], D)),
                          (b2[:, :], row(a["L0_gnn_b2"], D)), (b1[:, :], a["L0_gnn_b1"])])
        normalize(nc, c, "L0n", c.x, c.h, relu=True)

        def scale(dve, t, s, product):
            return dve.tensor_scalar(at(c.q, t)[:, 0:D], product[:, :], c.dinv[:, SRC, bass.ds(t, 1)] if not
                                     isinstance(t, int) else c.dinv[:, SRC, t:t + 1], None, ALU.mult)

        linear(nc, c, "L0p", c.h, w, D, scale, after=lambda sp, stored: store_table(sp, stored, c))
        gather_sum(nc, c, "L0s", SRC, c.rows256, c.acc, True)
        degree_scale(nc, c, "L0d", SRC, b, False)

        with Stage(nc, "L0o") as so:
            part, mid = so.sb("part", [P, 2, D]), so.sem("mid")

            def end(dve, t, s, product):
                dve.tensor_tensor(part[:, s, :], product[:, :], b2[:, :], ALU.add).then_inc(mid, 1)
                wait(dve, mid, t + 1)
                return dve.tensor_tensor(at(c.x, t), at(c.x, t), part[:, s, :], ALU.add)

            two_layers(nc, c, "L0m", c.h, w1, b1, 2, ACT.Relu, w2, end)


def store_table(sp, stored, c):
    sp.dma_start(c.rows256.rearrange("(b p) d -> p b d", p=P), c.q[:, :, 0:D]).then_inc(stored, 16)
    sp.wait_ge(stored, 16)


def degree_scale(nc, c, name, o, bias, residual):
    with Stage(nc, name) as st:
        done = st.sem("done")
        block = st.block()

        @block.vector
        def _(dve):
            count = [0]

            def then(instruction):
                count[0] += 1
                instruction.then_inc(done, 1)
                dve.wait_ge(done, count[0])

            then(dve.tensor_tensor(c.h[:, :, :], c.acc[:, :, 0:D], c.q[:, :, 0:D], ALU.add))
            then(dve.tensor_tensor(c.h[:, :, :], c.h[:, :, :], spread(c.dinv[:, o, :], 2, D), ALU.mult))
            then(dve.tensor_tensor(c.h[:, :, :], c.h[:, :, :], spread(bias[:, :], 1, NB), ALU.add))
            if residual:
                then(dve.tensor_scalar(c.h[:, :, :], c.h[:, :, :], 0.0, None, ALU.max))
                then(dve.tensor_tensor(c.x[:, :, :], c.x[:, :, :], c.h[:, :, :], ALU.add))


def layer1(nc, c, a):
    with Stage(nc, "L1") as st:
        w, b = st.sb("w", [P, 2, D]), st.sb("b", [P, D])
        fetch(nc, "L1w", [(w[:, :, :], matrix(a["L1_gnn_W"])), (b[:, :], row(a["L1_gnn_b"], D))])
        normalize(nc, c, "L1n", c.x, c.h, relu=True)

        def scale(dve, t, s, product):
            return dve.tensor_scalar(at(c.q, t)[:, 0:D], product[:, :], c.dinv[:, DST, bass.ds(t, 1)] if not
                                     isinstance(t, int) else c.dinv[:, DST, t:t + 1], None, ALU.mult)

        linear(nc, c, "L1p", c.h, w, D, scale, after=lambda sp, stored: store_table(sp, stored, c))
        gather_sum(nc, c, "L1s", DST, c.rows256, c.acc, False)
        degree_scale(nc, c, "L1d", DST, b, True)


def queries_keys_values(nc, c, a, layer, mask):
    types, kinds = a["L2_gnn_W_Q"].shape[1], a["L2_gnn_W_E"].shape[1]
    table = c.kv_rows.rearrange("(y n) w -> n y w", y=kinds)
    with Stage(nc, f"qkv{layer}") as st:
        wqv, wk = st.sb("wqv", [P, 2, types, 2, P]), st.sb("wk", [P, 2, types, P])
        we, scale = st.sb("we", [P, 2, kinds, P]), st.sb("scale", [P, 2, kinds])
        cleared, landed, scaled = st.sem("cleared"), st.sem("landed"), st.sem("scaled")
        with nc.Block() as block:
            @block.vector
            def _(dve):
                dve.memset(wqv[:, :, :, :, :], 0.0)
                dve.memset(wk[:, :, :, :], 0.0)
                dve.memset(we[:, :, :, :], 0.0).then_inc(cleared, 1)
                dve.wait_ge(landed, 16 * 5 * H)
                dve.tensor_scalar(scale[:, :, :], scale[:, :, :], float(HD) ** -0.5, None, ALU.mult).then_inc(scaled, 1)
                dve.wait_ge(scaled, 1)
                dve.tensor_tensor(we[:, :, :, :], we[:, :, :, :], spread(scale[:, :, :], 3, P), ALU.mult)

            @block.sync
            def _(sp):
                sp.wait_ge(cleared, 1)
                for h in range(H):
                    half, r = h // 4, slice(h % 4 * HD, (h % 4 + 1) * HD)
                    for to, name in ((wqv[r, half, :, 0, r], "W_Q"), (wqv[r, half, :, 1, r], "W_V"),
                                     (wk[r, half, :, r], "W_K"), (we[r, half, :, r], "W_E")):
                        sp.dma_start(to, a[f"L2_gnn_{name}"][layer, :, h, :, :].rearrange("t d e -> d t e")
                                     ).then_inc(landed, 16)
                    sp.dma_start(scale[r, half, :], a["L2_gnn_mu"][layer, h:h + 1, :].broadcast_to([HD, kinds])
                                 ).then_inc(landed, 16)

        here = [st.sb(f"here{s}", [P, types, D]) for s in range(2)]
        turned = [st.sb(f"turned{s}", [P, types, 2, P]) for s in range(2)]
        key_t = [st.sb(f"key_t{s}", [P, 2, P]) for s in range(2)]
        key_rows = [st.sb(f"key_rows{s}", [P, kinds, D]) for s in range(2)]
        value_rows = [st.sb(f"value_rows{s}", [P, VC]) for s in range(2)]
        flips = st.ps("flips", [P, types, 2, P])
        both = [st.ps(f"both{s}", [P, 2, 2, P]) for s in range(2)]
        key_ps, typed_ps = st.ps("key_ps", [P, 2, P]), st.ps("typed_ps", [P, 2, 512])
        here_ready, flipped, turned_ready, both_ready, key_ready, key_copied, typed_ready, rows_ready, values_ready = (
            st.sem(x) for x in ("here_ready", "flipped", "turned_ready", "both_ready", "key_ready", "key_copied",
                                "typed_ready", "rows_ready", "values_ready"))
        stored = [st.sem(f"stored{s}") for s in range(2)]
        puts = 1 + kinds
        block = st.block()

        def lagged(early, late):
            def run(eng):
                for t in range(4):
                    early(t, t % 2, t // 2)
                    if t:
                        late(t - 1, (t - 1) % 2, (t - 1) // 2)
                with eng.Fori(2, NB // 2) as i:
                    early(i * 2, 0, i)
                    late(i * 2 - 1, 1, i - 1)
                    early(i * 2 + 1, 1, i)
                    late(i * 2, 0, i)
                early(NB - 1, 0, NB // 2)
                late(NB - 2, 1, NB // 2 - 1)
                late(NB - 1, 0, NB // 2)
            return run

        def first(t):
            return isinstance(t, int) and t < 2

        @block.vector
        def _(dve):
            def part(t, s, i):
                if not first(t):
                    wait(dve, flipped, t - 1)
                for y in range(types):
                    factor = mask[:, y, bass.ds(t, 1)] if not isinstance(t, int) else mask[:, y, t:t + 1]
                    last = dve.tensor_scalar(here[s][:, y, :], at(c.h, t), factor, None, ALU.mult)
                last.then_inc(here_ready, 1)

            def end(t, s, i):
                wait(dve, both_ready, t + 1)
                if not first(t):
                    wait(dve, stored[s], i * (16 * puts))
                dve.tensor_copy(at(c.q, t)[:, 0:D].rearrange("p (a e) -> p a e", a=2), both[s][:, :, 0, :])
                dve.tensor_copy(
                    value_rows[s][:, :].rearrange("p (a h d) -> p a h d", a=2, h=H // 2)[:, :, :, 0:HD],
                    both[s][:, :, 1, :].rearrange("p a (h d) -> p a h d", h=H // 2)).then_inc(values_ready, 1)

            dve.memset(value_rows[0][:, :], 1.0).then_inc(values_ready, 1)
            dve.memset(value_rows[1][:, :], 1.0).then_inc(values_ready, 1)
            dve.wait_ge(values_ready, 2)
            lagged(part, end)(dve)

        @block.scalar
        def _(act):
            def turn(t, s, i):
                wait(act, flipped, t + 1)
                for k in range(2):
                    y = slice(k * types // 2, (k + 1) * types // 2)
                    last = act.activation(turned[s][:, y, :, :], flips[:, y, :, :], ACT.Copy)
                last.then_inc(turned_ready, 1)
                wait(act, key_ready, t + 1)
                act.activation(key_t[s][:, :, :], key_ps[:, :, :], ACT.Copy).then_inc(key_copied, 1)
                wait(act, typed_ready, t + 1)
                if not first(t):
                    wait(act, stored[s], i * (16 * puts))
                for k in range(2):
                    last = act.activation(key_rows[s][:, :, k * P:(k + 1) * P],
                                          typed_ps[:, k, 0:kinds * P].rearrange("p (y e) -> p y e", y=kinds), ACT.Copy)
                last.then_inc(rows_ready, 1)

            lagged(turn, lambda t, s, i: None)(act)

        @block.tensor
        def _(pe):
            def multiply(t, s, i):
                wait(pe, here_ready, t + 1)
                wait(pe, turned_ready, t + 1)
                for y in range(types):
                    for k in range(2):
                        last = pe.transpose(flips[:, y, k, :], here[s][:, y, k * P:(k + 1) * P], c.ident[:, :])
                last.then_inc(flipped, 1)
                wait(pe, turned_ready, t + 2)
                wait(pe, key_copied, t + 1)
                for k in range(2):
                    for y in range(types):
                        last = pe.matmul(key_ps[:, k, :], wk[:, k, y, :], turned[s][:, y, k, :], start=y == 0,
                                         stop=y == types - 1)
                last.then_inc(key_ready, 1)
                wait(pe, values_ready, t + 1)
                for k in range(2):
                    for y in range(types):
                        last = pe.matmul(both[s][:, k, :, :].rearrange("p a e -> p (a e)"), turned[s][:, y, k, :],
                                         wqv[:, k, y, :, :].rearrange("p a e -> p (a e)"), start=y == 0,
                                         stop=y == types - 1)
                last.then_inc(both_ready, 1)
                wait(pe, key_copied, t + 2)
                wait(pe, rows_ready, t + 1)
                for k in range(2):
                    last = pe.matmul(typed_ps[:, k, 0:kinds * P], key_t[s][:, k, :],
                                     we[:, k, :, :].rearrange("p y e -> p (y e)"), start=True, stop=True)
                last.then_inc(typed_ready, 1)

            for free in (turned_ready, key_copied, rows_ready):
                pe.sem_inc(free, 1)
            lagged(multiply, lambda t, s, i: None)(pe)

        @block.sync
        def _(sp):
            def put(t, s, i):
                nodes = bass.ds(t * P, P)
                wait(sp, rows_ready, t + 2)
                wait(sp, values_ready, t + 3)
                sp.dma_start(table[nodes, :, 0:D], key_rows[s][:, :, :]).then_inc(stored[s], 16)
                for y in range(kinds):
                    sp.dma_start(c.kv_rows[bass.ds(t * P + y * NP, P), D:D + VC], value_rows[s][:, :]
                                 ).then_inc(stored[s], 16)

            lagged(put, lambda t, s, i: None)(sp)
            sp.wait_ge(stored[0], 16 * puts * (NB // 2 + 1))
            sp.wait_ge(stored[1], 16 * puts * (NB // 2))


def divide(nc, c, name, floor, finish):
    with Stage(nc, name) as st:
        total = st.sb("total", [P, NB * H])
        done = st.sem("done")
        block = st.block()

        @block.vector
        def _(dve):
            count = [0]

            def then(instruction):
                count[0] += 1
                instruction.then_inc(done, 1)
                dve.wait_ge(done, count[0])

            heads = c.acc[:, :, :].rearrange("p b (h d) -> p (b h) d", h=H)
            then(dve.tensor_scalar(total[:, :], heads[:, :, HD], floor[1], None, floor[0]))
            then(dve.reciprocal(total[:, :], total[:, :]))
            then(dve.tensor_tensor(c.flat[:, :].rearrange("p (n d) -> p n d", d=HD), heads[:, :, 0:HD],
                                   spread(total[:, :], 2, HD), ALU.mult))
            finish(dve, then)


def add_product(c, bias, part, mid):
    def end(dve, t, s, product):
        dve.tensor_tensor(part[:, s, :], product[:, :], bias, ALU.add).then_inc(mid, 1)
        wait(dve, mid, t + 1)
        return dve.tensor_tensor(at(c.h, t), at(c.h, t), part[:, s, :], ALU.add)
    return end


def node_masks(nc, c, a, mask):
    with Stage(nc, "types") as st:
        kind_i, kind = st.sb("kind_i", [P, NB], I32), st.sb("kind", [P, NB])
        cleared, landed, made = st.sem("cleared"), st.sem("landed"), st.sem("made")
        block = st.block()
        full = N // P * P

        @block.sync
        def _(sp):
            sp.wait_ge(cleared, 1)
            sp.dma_start(kind_i[:, 0:NB - 1], a["node_type_4"]).then_inc(landed, 16)
            sp.dma_start(kind_i[0:N - full, NB - 1:NB], a["node_type_4_rest"]).then_inc(landed, 16)

        @block.vector
        def _(dve):
            dve.memset(kind_i[:, :], 0).then_inc(cleared, 1)
            dve.wait_ge(landed, 32)
            dve.tensor_copy(kind[:, :], kind_i[:, :]).then_inc(made, 1)
            dve.wait_ge(made, 1)
            for y in range(mask.shape[1]):
                dve.tensor_scalar(mask[:, y, :], kind[:, :], float(y), None, ALU.is_equal)


def park(nc, c, name, back):
    with Stage(nc, name) as st:
        moved = st.sem("moved")
        block = st.block()

        @block.sync
        def _(sp):
            chip, dram = c.x[:, :, :], c.parked.rearrange("(b p) d -> p b d", p=P)
            sp.dma_start(*((chip, dram) if back else (dram, chip))).then_inc(moved, 16)
            sp.wait_ge(moved, 16)


def layer2(nc, c, a):
    with Stage(nc, "L2") as st:
        types, layers = a["L2_gnn_W_Q"].shape[1], a["L2_gnn_W_Q"].shape[0]
        mask = st.sb("mask", [P, types, NB])
        node_masks(nc, c, a, mask)
        normalize(nc, c, "L2n", c.x, c.h, relu=True)
        park(nc, c, "L2p", False)
        c.q, c.flat = c.x, c.x[:, :, :].rearrange("p b d -> p (b d)")
        for l in range(layers):
            queries_keys_values(nc, c, a, l, mask)
            attend(nc, c, f"L2a{l}", c.kv_rows, D + VC, D, True)
            divide(nc, c, f"L2v{l}", (ALU.add, 1e-10), lambda dve, then: None)
            with Stage(nc, f"L2w{l}") as sw:
                wo, rows = sw.sb("wo", [P, 2, D]), sw.sb("rows", [P, 6, D])
                w1, w2, b1 = sw.sb("w1", [P, 2, 4 * D]), sw.sb("w2", [P, 8, D]), sw.sb("b1", [P, 8])
                part = sw.sb("part", [P, 2, D])
                fetch(nc, f"L2f{l}", [(wo[:, :, :], matrix(a["L2_gnn_Wo"][l])),
                                      (w1[:, :, :], matrix(a["L2_gnn_w1"][l])),
                                      (w2[:, :, :], a["L2_gnn_w2"][l].rearrange("(j p) n -> p j n", p=P)),
                                      (b1[:, :], a["L2_gnn_b1"][l])] +
                      [(rows[:, k, :], row(a[f"L2_gnn_{name}"][l], D)) for k, name in
                       enumerate(("bo", "ln1_g", "ln1_b", "b2", "ln2_g", "ln2_b"))])
                linear(nc, c, f"L2o{l}", c.q, wo, D, add_product(c, rows[:, 0, :], part, sw.sem("mid0")))
                normalize(nc, c, f"L2x{l}", c.h, c.h, gain=rows[:, 1, :], bias=rows[:, 2, :])
                two_layers(nc, c, f"L2m{l}", c.h, w1, b1, 8, ACT.Gelu, w2,
                           add_product(c, rows[:, 3, :], part, sw.sem("mid1")))
                normalize(nc, c, f"L2y{l}", c.h, c.h, gain=rows[:, 4, :], bias=rows[:, 5, :])
        park(nc, c, "L2q", True)
        rows = st.sb("rows", [P, 2, D])
        fetch(nc, "L2g", [(rows[:, 0, :], row(a["L2_gnn_out_g"], D)), (rows[:, 1, :], row(a["L2_gnn_out_b"], D))])
        normalize(nc, c, "L2z", c.h, c.h, gain=rows[:, 0, :], bias=rows[:, 1, :], add_to=c.x)


def layer3(nc, c, a):
    c.q = c.h
    with Stage(nc, "L3") as st:
        w, ends = st.sb("w", [P, 2, D]), st.sb("ends", [P, 2, D])
        part, mid = st.sb("part", [P, 2, 2, D]), st.sem("mid")
        fetch(nc, "L3w", [(w[:, :, :], matrix(a["L3_gnn_W"])),
                          (ends[:, 0, :], row(a["L3_gnn_a_src"].rearrange("h d -> (h d)"), D)),
                          (ends[:, 1, :], row(a["L3_gnn_a_dst"].rearrange("h d -> (h d)"), D))])
        normalize(nc, c, "L3n", c.x, c.h, relu=True)
        with Stage(nc, "L3o") as sx:
            block = sx.block()

            @block.vector
            def _(dve):
                dve.memset(c.acc[:, :, :], 1.0)

        def end(dve, t, s, product):
            dve.tensor_copy(at(c.h, t), product[:, :])
            dve.tensor_copy(at(c.acc, t).rearrange("p (h d) -> p h d", h=H)[:, :, 0:HD],
                            product[:, :].rearrange("p (h d) -> p h d", h=H))
            dve.tensor_tensor(part[:, s, :, :], spread(product[:, :], 1, 2), ends[:, :, :], ALU.mult
                              ).then_inc(mid, 1)
            wait(dve, mid, t + 1)
            heads = part[:, s, :, :].rearrange("p a (h d) -> p a h d", h=H)
            dve.tensor_reduce(at(c.top, t), heads[:, 0, :, :], AX.X, ALU.add)
            return dve.tensor_reduce(at(c.ends, t), heads[:, 1, :, :], AX.X, ALU.add)

        def store(sp, stored):
            rows = c.feature_rows.rearrange("(b p) d -> p b d", p=P)
            sp.dma_start(rows[:, :, 0:VC], c.acc[:, :, :]).then_inc(stored, 16)
            sp.dma_start(rows[:, :, VC:VC + H], c.top[:, :, :]).then_inc(stored, 16)
            sp.wait_ge(stored, 32)

        linear(nc, c, "L3p", c.h, w, D, end, after=store)
    with Stage(nc, "L3e") as st:
        encode = st.sb("encode", [GT * EF, GT, D])
        with Stage(nc, "L3c") as so:
            cleared, landed = so.sem("cleared"), so.sem("landed")
            block = so.block()

            @block.vector
            def _(dve):
                dve.memset(encode[:, :, :], 0.0).then_inc(cleared, 1)

            @block.sync
            def _(sp):
                sp.wait_ge(cleared, 1)
                for u in range(GT):
                    sp.dma_start(encode[u * EF + 4:u * EF + 7, u, :], a["L3_gnn_edge_W"]).then_inc(landed, 16)
                    sp.dma_start(encode[u * EF + 7:u * EF + 8, u, :], a["L3_gnn_edge_b"].rearrange("(a n) -> a n", a=1)
                                 ).then_inc(landed, 16)
                sp.wait_ge(landed, 16 * 2 * GT)

        attend(nc, c, "L3a", c.feature_rows, VC + H, 0, False, encode)
    with Stage(nc, "L3b") as st:
        bias = st.sb("bias", [P, D])
        fetch(nc, "L3d", [(bias[:, :], row(a["L3_gnn_bias"], D))])
        c.flat = c.h[:, :, :].rearrange("p b d -> p (b d)")

        def finish(dve, then):
            then(dve.tensor_tensor(c.h[:, :, :], c.h[:, :, :], spread(bias[:, :], 1, NB), ALU.add))
            then(dve.tensor_tensor(c.x[:, :, :], c.x[:, :, :], c.h[:, :, :], ALU.add))

        divide(nc, c, "L3v", (ALU.max, 1e-10), finish)


def program(nc, a, out):
    c = Buffers()
    with ExitStack() as ctx:
        def sb(name, shape, dt=F32):
            return ctx.enter_context(nc.sbuf_tensor(name, shape, dt))

        c.ident, c.count = sb("ident", [P, P]), sb("count", [P, P])
        c.x = sb("x", [P, NB, D])
        c.dinv = sb("dinv", [P, 2, NB])
        c.block, c.block_i = sb("block", [P, 2, NPR]), sb("block_i", [P, 2, NPR + 3 * GP], I32)
        c.local, c.index = sb("local", [P, 2, NT]), sb("index", [P, 2, NT], I32)
        c.weight, c.typed_index = sb("weight", [P, NT]), sb("typed_index", [P, NT], I32)
        c.last, c.fresh = sb("last", [P, NT]), sb("fresh", [P, NT])
        c.meta = sb("meta", [P, NT, EF])
        c.edge_rows = nc.dram_tensor("edge_rows", [ER, EF], F32, kind="Internal").ap()
        c.source_rows = nc.dram_tensor("source_rows", [NPR * PAIR + ER - E, SF], F32, kind="Internal").ap()
        c.kv_rows = nc.dram_tensor("kv_rows", [3 * NP, D + VC], F32, kind="Internal").ap()
        c.feature_rows = nc.dram_tensor("feature_rows", [NP, VC + H], F32, kind="Internal").ap()
        c.parked = nc.dram_tensor("parked", [NP, D], F32, kind="Internal").ap()
        c.rows256 = nc.dram_tensor("rows256", [NP, D], F32, kind="Internal").ap()
        with ExitStack() as prep:
            def psb(name, shape, dt=F32):
                return prep.enter_context(nc.sbuf_tensor(name, shape, dt))

            c.down, c.up, c.zeros, c.ones, c.upper = (
                psb(name, [P, P]) for name in ("down", "up", "zeros", "ones", "upper"))
            c.turns, c.edge = psb("turns", [P, NPR]), psb("edge", [P, T])
            c.pack, c.first = psb("pack", [P, T, EF]), psb("first", [P, 2, NB + 1])
            c.start_i, c.before = psb("start_i", [P, NPR], I32), psb("before", [P, 2, NB + 1])
            c.place, c.by_source = psb("place", [P, T], I32), psb("by_source", [P, T, SF])
            constants(nc, c)
            load_edges(nc, c, a)
            rank_sources(nc, c)
            scatter_sources(nc, c)
            load_pairs(nc, c)
        c.h, c.acc, c.top = sb("h", [P, NB, D]), sb("acc", [P, NB, VC]), sb("top", [P, NB, H])
        load_nodes(nc, c, a["x"])
        with nc.sbuf_tensor("features", [P, NB, D], F32) as c.q:
            layer0(nc, c, a)
            layer1(nc, c, a)
        layer2(nc, c, a)
        with nc.sbuf_tensor("ends", [P, NB, H], F32) as c.ends:
            layer3(nc, c, a)
        store_nodes(nc, c, out)





def load_nodes(nc, c, x):
    with Stage(nc, "load") as st:
        cleared, landed = st.sem("cleared"), st.sem("landed")
        block = st.block()

        @block.vector
        def _(dve):
            dve.memset(c.x[:, NB - 1, :], 0.0).then_inc(cleared, 1)

        @block.sync
        def _(sp):
            full = N // P * P
            sp.dma_start(c.x[:, 0:NB - 1, :], x[0:full, :].rearrange("(b p) d -> p b d", p=P)).then_inc(landed, 16)
            sp.wait_ge(cleared, 1)
            sp.dma_start(c.x[0:N - full, NB - 1, :], x[full:N, :]).then_inc(landed, 16)
            sp.wait_ge(landed, 32)


def store_nodes(nc, c, out):
    with Stage(nc, "store") as st:
        stored = st.sem("stored")
        block = st.block()

        @block.sync
        def _(sp):
            full = N // P * P
            sp.dma_start(out[0:full, :].rearrange("(b p) d -> p b d", p=P), c.x[:, 0:NB - 1, :]).then_inc(stored, 16)
            sp.dma_start(out[full:N, :], c.x[0:N - full, NB - 1, :]).then_inc(stored, 16)
            sp.wait_ge(stored, 32)


def kernel(**inputs):
    import numpy as np
    import concourse.bacc as bacc
    from concourse.bass_utils import run_bass_kernel_spmd

    nc = bacc.Bacc("TRN2", target_bir_lowering=False, num_devices=1)
    arrays, a = {}, {}
    for name, value in inputs.items():
        value = np.asarray(value)
        if name == "L3_gnn_W" or name == "L3_gnn_edge_W":
            value = value.T
        if name == "L0_gnn_b1":
            value = value.reshape(2, P).T
        if name == "L2_gnn_b1":
            value = value.reshape(3, 8, P).transpose(0, 2, 1)
        if name == "node_type_4":
            full = N // P * P
            rest, value = np.ascontiguousarray(value[full:].reshape(-1, 1)), value[:full].reshape(-1, P).T
            arrays["rest_in"] = rest
            a["node_type_4_rest"] = nc.dram_tensor("rest_in", rest.shape, I32, kind="ExternalInput").ap()
        value = np.ascontiguousarray(value)
        arrays[f"{name}_in"] = value
        a[name] = nc.dram_tensor(f"{name}_in", value.shape, mybir.dt.from_np(value.dtype), kind="ExternalInput").ap()
    out = nc.dram_tensor("out", (N, D), F32, kind="ExternalOutput").ap()
    program(nc, a, out)
    return run_bass_kernel_spmd(nc, [arrays], core_ids=[0]).results[0]["out"]
```
